# Optimizing a Trainium2 kernel written in Bass

```python
import numpy as np
import jax
import jax.numpy as jnp

def _softmax(x, axis=-1):
    return jax.nn.softmax(x, axis=axis)

def _gelu(x):
    return jax.nn.gelu(x, approximate=True)

def _silu(x):
    return jax.nn.silu(x)

def _sigmoid(x):
    return jax.nn.sigmoid(x)

def _layernorm(x, axis=-1, eps=1e-05):
    m = jnp.mean(x, axis=axis, keepdims=True)
    v = jnp.var(x, axis=axis, keepdims=True)
    return (x - m) / jnp.sqrt(v + eps)

def _scatter_add(tgt, idx, src, axis=0):
    return tgt.at[idx].add(src)

def _segment_sum(src, seg, n):
    return jax.ops.segment_sum(src, seg, n)
kernel_name = 'mk_gnn_preln_d1_gnn_r8_cea355'

def setup_inputs(seed: int=0):
    np.random.seed(seed)
    _w = jnp.asarray

    def _rec_inputs():
        import jax
        import jax.numpy as jnp
        _gk = jax.random.key(seed)
        x = -0.0005121 + 1.001 * jax.random.normal(jax.random.fold_in(_gk, 1), (6250, 64), jnp.float32)
        _s = jax.random.randint(jax.random.fold_in(_gk, 2), (100000,), 0, 6250, jnp.int32)
        _d = jax.random.randint(jax.random.fold_in(_gk, 3), (100000,), 0, 6250, jnp.int32)
        _loop = jnp.arange(6250, dtype=jnp.int32)
        src = jnp.concatenate([_s, _d, _loop])
        dst = jnp.concatenate([_d, _s, _loop])
        _o = jnp.argsort(dst, stable=True)
        src = src[_o]
        dst = dst[_o]
        edge_attr_64 = 0.000189758 + 1.00013 * jax.random.normal(jax.random.fold_in(_gk, 12), (206250, 64), jnp.float32)
        return (x, src, dst, edge_attr_64)
    x, src, dst, edge_attr_64 = _rec_inputs()

    def _L0_gnn_setup():
        import jax, jax.numpy as jnp
        import numpy as np
        N_NODES = 6250
        N_EDGES = 100000
        D_NODE = 64
        D_EDGE = 64
        D_H = 128
        D_U = 32
        D_OUT = 64
        N_GRAPHS = 16
        key = jax.random.key(seed)
        ks = jax.random.split(key, 16)
        x = jax.random.normal(ks[0], (N_NODES, D_NODE), dtype=jnp.float32)
        edge_index = jax.random.randint(ks[1], (2, N_EDGES), 0, N_NODES, dtype=jnp.int64)
        edge_attr = jax.random.normal(ks[2], (N_EDGES, D_EDGE), dtype=jnp.float32)
        u = jax.random.normal(ks[3], (N_GRAPHS, D_U), dtype=jnp.float32)
        batch = jnp.sort(jax.random.randint(ks[4], (N_NODES,), 0, N_GRAPHS, dtype=jnp.int64))
        s = 0.05
        W1 = jax.random.normal(ks[5], (D_H, D_NODE + D_EDGE), dtype=jnp.float32) * s
        b1 = jax.random.normal(ks[6], (D_H,), dtype=jnp.float32) * s
        W2 = jax.random.normal(ks[7], (D_H, D_H), dtype=jnp.float32) * s
        b2 = jax.random.normal(ks[8], (D_H,), dtype=jnp.float32) * s
        Wa = jax.random.normal(ks[9], (D_H, D_NODE + D_H + D_U), dtype=jnp.float32) * s
        ba = jax.random.normal(ks[10], (D_H,), dtype=jnp.float32) * s
        Wb = jax.random.normal(ks[11], (D_OUT, D_H), dtype=jnp.float32) * s
        bb = jax.random.normal(ks[12], (D_OUT,), dtype=jnp.float32) * s
        return {'x': x, 'edge_index': edge_index, 'edge_attr': edge_attr, 'u': u, 'batch': batch, 'W1': W1, 'b1': b1, 'W2': W2, 'b2': b2, 'Wa': Wa, 'ba': ba, 'Wb': Wb, 'bb': bb}
    _L0_gnn_all = _L0_gnn_setup()
    _L0_gnn_in = {k: v for k, v in _L0_gnn_all.items() if k in ('u', 'W1', 'b1', 'W2', 'b2', 'Wa', 'ba', 'Wb', 'bb')}
    del _L0_gnn_all
    return {'x': x, 'src': src, 'dst': dst, 'edge_attr_64': edge_attr_64, 'L0_gnn_u': _L0_gnn_in['u'], 'L0_gnn_W1': _L0_gnn_in['W1'], 'L0_gnn_b1': _L0_gnn_in['b1'], 'L0_gnn_W2': _L0_gnn_in['W2'], 'L0_gnn_b2': _L0_gnn_in['b2'], 'L0_gnn_Wa': _L0_gnn_in['Wa'], 'L0_gnn_ba': _L0_gnn_in['ba'], 'L0_gnn_Wb': _L0_gnn_in['Wb'], 'L0_gnn_bb': _L0_gnn_in['bb']}

def reference(x, src, dst, edge_attr_64, L0_gnn_u, L0_gnn_W1, L0_gnn_b1, L0_gnn_W2, L0_gnn_b2, L0_gnn_Wa, L0_gnn_ba, L0_gnn_Wb, L0_gnn_bb):
    import jax
    import jax.numpy as jnp

    def _L0_gnn_ref(x, edge_index, edge_attr, u, batch, W1, b1, W2, b2, Wa, ba, Wb, bb):
        import jax, jax.numpy as jnp
        import numpy as np
        N_NODES = 6250
        N_EDGES = 100000
        D_NODE = 64
        D_EDGE = 64
        D_H = 128
        D_U = 32
        D_OUT = 64
        N_GRAPHS = 16
        row, col = (edge_index[0], edge_index[1])
        h = jnp.concatenate([x[col], edge_attr], axis=1)
        h = jax.nn.relu(h @ W1.T + b1)
        h = jax.nn.relu(h @ W2.T + b2)
        n = x.shape[0]
        summed = jax.ops.segment_sum(h, row, num_segments=n)
        cnt = jax.ops.segment_sum(jnp.ones((h.shape[0],), dtype=h.dtype), row, num_segments=n)
        agg = summed / jnp.maximum(cnt, 1.0)[:, None]
        z = jnp.concatenate([x, agg, u[batch]], axis=1)
        z = jax.nn.relu(z @ Wa.T + ba)
        return z @ Wb.T + bb
    edge_index = jnp.stack([src, dst])
    batch0 = jnp.zeros((6250,), jnp.int32)
    h = jnp.maximum(_layernorm(x, axis=-1), 0.0)
    x = x + _L0_gnn_ref(h, edge_index, edge_attr_64, L0_gnn_u, batch0, L0_gnn_W1, L0_gnn_b1, L0_gnn_W2, L0_gnn_b2, L0_gnn_Wa, L0_gnn_ba, L0_gnn_Wb, L0_gnn_bb)
    return x

_drawn_inputs = setup_inputs


def setup_inputs(seed=0):
    import zlib

    import numpy as np

    out = dict(_drawn_inputs(seed))
    spreads = {}
    factors = {'edge_attr_64': 8.0,
     'L0_gnn_W1': 7.856,
     'L0_gnn_b1': 37.884,
     'L0_gnn_W2': 3.677,
     'L0_gnn_b2': 37.737,
     'L0_gnn_ba': 8.0,
     'L0_gnn_bb': 4.922}
    for name, (base, spread) in spreads.items():
        noise = np.random.default_rng([zlib.crc32(name.encode()), seed]).standard_normal(out[name].shape)
        drawn = base * np.exp(spread * noise) if base else spread * noise
        out[name] = jnp.asarray(drawn.astype(out[name].dtype))
    for name, factor in factors.items():
        out[name] = (out[name] * factor).astype(out[name].dtype)
    return out
```

```python
import concourse.bass as bass
from concourse import mybir
from contextlib import ExitStack

N, E, D, H, DU = 6250, 206250, 64, 128, 32
P = 128
TILE = 128
TPG = 4
GE = TILE * TPG
UNROLL = 8
STEPS = -(-E // (GE * UNROLL))
NG = STEPS * UNROLL
NT = NG * TPG
WIN = 64
SELP = 64
RB = -(-N // (P * 4)) * 4
NROWS = P * RB
RCH = 4
NCH = RB // RCH
C = H + 1
SCRAP = N
NSETS = 8
EPS = 1e-5
assert STEPS <= SELP and N + P < NROWS and N + WIN <= NROWS


def build(nc, x, src_cols, dst_cols, src_rows, dst_rows, ea, u, w1t, b1, w2t, b2, wat, ba, wbt, bb, out):
    f32, bf16, i32 = mybir.dt.float32, mybir.dt.bfloat16, mybir.dt.int32
    ALU = mybir.AluOpType
    ACT = mybir.ActivationFunctionType
    AX = mybir.AxisListType
    ds = bass.ds

    table = nc.dram_tensor("p_table", (NROWS, H), f32, kind="Internal").ap()
    sums = [nc.dram_tensor(f"sums{k}", (NROWS, C), f32, kind="Internal").ap() for k in range(NSETS)]

    ctx = ExitStack()
    with ctx:
        def sb(name, shape, dt):
            return ctx.enter_context(nc.sbuf_tensor(name, shape, dt))

        def sem(name):
            return ctx.enter_context(nc.semaphore(name))

        x_sb = sb("x_sb", [P, RB, D], f32)
        h_sb = sb("h_sb", [P, RB, D], f32)
        o_sb = h_sb
        hT = sb("hT", [D, NROWS], f32)
        regA = sb("regA", [P, max(RB * H, 4 * 2 * GE + 4 * TPG * C + 2 * TPG * H)], f32)
        sq = regA[:, 0:RB * D].rearrange("p (r f) -> p r f", f=D)
        p_sb = regA[:, 0:RB * H].rearrange("p (r f) -> p r f", f=H)
        R = regA[:, 0:4 * 2 * GE].rearrange("p (q e) -> p q e", q=UNROLL)
        o1 = 4 * 2 * GE
        scat = regA[:, o1:o1 + 4 * TPG * C].rearrange("p (s t c) -> p s t c", s=4, c=C)
        o2 = o1 + 4 * TPG * C
        X = regA[:, o2:o2 + 2 * TPG * H].rearrange("p (s t f) -> p s t f", s=2, f=H)
        RW = UNROLL * GE
        KC = RCH * C
        regB = sb("regB", [P, max(2 * RW, 2 * NSETS * KC)], f32)
        src_ri = regB[:, 0:RW].bitcast(i32).rearrange("p (b e) -> p b e", e=GE)
        dst_rf = regB[:, RW:2 * RW].rearrange("p (b e) -> p b e", e=GE)
        dst_ri = dst_rf.bitcast(i32)
        SA = regB[:, 0:2 * NSETS * KC].rearrange("p (s k c) -> p s k c", s=2, k=NSETS)
        srcR = sb("srcR", [P, UNROLL, GE], bf16)
        dstR = sb("dstR", [P, UNROLL, GE], bf16)
        dst0 = sb("dst0", [SELP, UNROLL], f32)
        srcI = sb("srcI", [P, NT], i32)
        srcF = sb("srcF", [P, NT], f32)
        toscrap = sb("toscrap", [P, NT], f32)
        dstI = sb("dstI", [P, NT], i32)
        base = sb("base", [1, SELP * UNROLL], i32)
        L = sb("L", [P, UNROLL, H], f32)
        S = sb("S", [P, 4, TPG, TILE], f32)
        h1 = sb("h1", [P, 2, GE], f32)
        h2 = sb("h2", [P, 2, TPG, C], f32)
        cnt = sb("cnt", [P, UNROLL, TPG], f32)
        extra = sb("extra", [P, 2, TPG], f32)
        idx = sb("idx", [P, UNROLL, TPG], i32)
        gidx = sb("gidx", [P, 2, TPG], i32)
        zeros = sb("zeros", [P, C * 10], f32)
        ident = sb("ident", [P, P], f32)
        tri = sb("tri", [P, P], f32)
        onesf = sb("onesf", [P, P], f32)
        onesb = sb("onesb", [P, P], bf16)
        sel = sb("sel", [P, SELP], bf16)
        winrow = sb("winrow", [P, 1], f32)
        scrapc = sb("scrapc", [P, 1], f32)
        epsc = sb("epsc", [P, 1], f32)
        w1x = sb("w1x", [D, H], f32)
        w2 = sb("w2", [H, H], f32)
        wax = sb("wax", [D, H], f32)
        waa = sb("waa", [H, H], f32)
        wau = sb("wau", [DU, H], f32)
        wb = sb("wb", [H, D], f32)
        u0 = sb("u0", [DU, 1], f32)
        b1b = sb("b1b", [P, H], f32)
        b2b = sb("b2b", [P, H], f32)
        b2w = sb("b2w", [P, 2, H], f32)
        b2p = sb("b2p", [P, 3, H], bf16)
        b2R = sb("b2R", [P, TPG, H], bf16)
        bac = sb("bac", [H, 1], f32)
        biasz = sb("biasz", [H, 1], f32)
        bbb = sb("bbb", [P, D], f32)
        stat = sb("stat", [P, 4, RB], f32)
        viol = sb("viol", [P, 6], f32)
        mode = sb("mode", [1, 1], i32)
        rc = sb("rc", [P, 2, RCH], f32)

        def take(width, at=[0]):
            at[0] += width
            return regA[:, at[0] - width:at[0]]

        s4, s2, s1 = take(4 * KC), take(2 * KC), take(KC)
        agg = take(2 * GE).rearrange("p (s r f) -> p s r f", s=2, f=H)
        aggT = take(2 * GE).rearrange("p (s e) -> p s e", s=2)
        zT = take(2 * GE).rearrange("p (s e) -> p s e", s=2)

        bank = ctx.enter_context(nc.psum_tensor("bank", [P, 8, 512], f32))
        psDst, psSrc = bank[:, 0, :], bank[:, 1, :]

        def psL1(s):
            return bank[:, 2 + s, :]

        def psL2(s):
            return bank[:, 4 + s, :]

        psSum = bank[:, 6:8, 0:2 * C]

        x_in = sem("x_in")
        rows_in = sem("rows_in")
        cols_in = sem("cols_in")
        base_in = sem("base_in")
        w_in = sem("w_in")
        wz_in = sem("wz_in")
        consts = sem("consts")
        zeroed = sem("zeroed")
        sums_zeroed = [sem(f"sums_zeroed{k}") for k in range(NSETS)]
        dve_step = sem("dve_step")
        act_step = sem("act_step")
        ln_centred = sem("ln_centred")
        ln_squared = sem("ln_squared")
        ln_var = sem("ln_var")
        ln_std = sem("ln_std")
        h_ready = sem("h_ready")
        hT_psum = sem("hT_psum")
        hT_ready = sem("hT_ready")
        p_psum = sem("p_psum")
        p_ready = sem("p_ready")
        table_stored = sem("table_stored")
        viol_ready = sem("viol_ready")
        viol_sum = sem("viol_sum")
        mode_ready = sem("mode_ready")
        src_masked = sem("src_masked")
        srcR_ready = sem("srcR_ready")
        tables_ready = sem("tables_ready")
        x_used = sem("x_used")
        xbb_ready = sem("xbb_ready")
        zb_psum = sem("zb_psum")
        biasz_ready = sem("biasz_ready")

        ea_in = [sem(f"ea_in{q}") for q in range(4)]
        win_in = [sem(f"win_in{q}") for q in range(UNROLL)]
        bcast_done = sem("bcast_done")
        oh_ready = sem("oh_ready")
        mask_ready = sem("mask_ready")
        extra_ready = sem("extra_ready")
        idx_ready = sem("idx_ready")
        l1_done = sem("l1_done")
        h1_ready = sem("h1_ready")
        l2_done = sem("l2_done")
        h2_ready = sem("h2_ready")
        sum_done = sem("sum_done")
        scat_ready = sem("scat_ready")
        added = [sem(f"added{k}") for k in range(NSETS)]
        gidx_ready = sem("gidx_ready")
        gathered = [sem(f"gathered{s}") for s in range(2)]

        acc_in = [sem(f"acc_in{s}") for s in range(2)]
        s4_done = sem("s4_done")
        agg_ready = sem("agg_ready")
        aggT_psum = sem("aggT_psum")
        aggT_ready = sem("aggT_ready")
        z_psum = sem("z_psum")
        z_ready = sem("z_ready")
        o_psum = sem("o_psum")
        o_ready = sem("o_ready")
        stored = sem("stored")

        block = ctx.enter_context(nc.Block())

        def live(i, j):
            return not isinstance(i, int) or 0 <= UNROLL * i + j < NG

        def wait(eng, s, value):
            if not isinstance(value, int) or value > 0:
                eng.wait_ge(s, value)

        def run_steps(eng, step, lead, lag):
            for j in range(-lead, UNROLL):
                step(0, j)
            with eng.Fori(1, STEPS - 1) as i:
                for j in range(UNROLL):
                    step(i, j)
            for j in range(UNROLL + lag):
                step(STEPS - 1, j)

        @block.sync
        def _(sp):
            sp.dma_start(x_sb[:, :, :], x.rearrange("(p r) f -> p r f", p=P)).then_inc(x_in, 16)
            sp.dma_start(dst_ri[0:SELP, :, :], dst_rows).then_inc(rows_in, 16)
            sp.dma_start(src_ri[0:SELP, :, :], src_rows).then_inc(rows_in, 16)
            sp.dma_start(src_ri[SELP:P, :, :], src_rows).then_inc(rows_in, 16)
            sp.dma_start(w1x[:, :], w1t[0:D, :]).then_inc(w_in, 16)
            sp.dma_start(b1b[:, :], b1.partition_broadcast(P)).then_inc(w_in, 16)
            sp.dma_start(b2b[:, :], b2.partition_broadcast(P)).then_inc(w_in, 16)
            sp.dma_start(w2[:, :], w2t).then_inc(w_in, 16)
            sp.dma_start(L[0:D, :, :], w1t[D:2 * D, :].unsqueeze(1).broadcast_to([D, UNROLL, H])).then_inc(w_in, 16)
            sp.dma_start(srcI[:, :], src_cols).then_inc(cols_in, 16)
            sp.dma_start(dstI[:, :], dst_cols).then_inc(cols_in, 16)
            with nc.allow_non_contiguous_dma("first dst of each group"):
                sp.dma_start(base[0:1, :], dst_rows[:, :, 0:1].rearrange("(a s) b o -> a (s b o)", a=1)).then_inc(base_in, 16)
            sp.wait_ge(p_ready, NCH)
            sp.dma_start(table.rearrange("(p r) f -> p r f", p=P), p_sb).then_inc(table_stored, 16)
            sp.wait_ge(table_stored, 16)
            sp.wait_ge(base_in, 16)
            sp.wait_ge(w_in, 16 * 5)

            def step(i, j):
                if not live(i, j):
                    return
                g = UNROLL * i + j
                if j % 2 == 0:
                    wait(sp, l1_done, g - UNROLL + 2)
                    sp.dma_start(R[0:D, j:j + 2, :], ea[ds(4 * i + j // 2, 1)].rearrange("o f (q e) -> (o f) q e", q=2)).then_inc(ea_in[j // 2], 16)
                wait(sp, l1_done, g - UNROLL + 1)
                row = sp.value_load(base[0:1, ds(g, 1)], min_val=0, max_val=N - 1)
                sp.dma_start(L[D:P, j, :], table[ds(row, WIN), :]).then_inc(win_in[j], 16)

            run_steps(sp, step, 0, 0)

            for k in range(NSETS):
                sp.wait_ge(added[k], 16 * STEPS * UNROLL * TPG // NSETS)
            for c in range(NCH):
                if c >= 2:
                    sp.wait_ge(s4_done, c - 1)
                for k in range(NSETS):
                    sp.dma_start(SA[:, c % 2, k, :], sums[k].rearrange("(p r) c -> p (r c)", p=P)[:, c * KC:(c + 1) * KC]).then_inc(acc_in[c % 2], 16)
            out_v = out.rearrange("(p r) f -> p r f", p=P)
            for c in range(NCH):
                sp.wait_ge(o_ready, c + 1)
                sp.dma_start(out_v[:, RCH * c:RCH * (c + 1), :], o_sb[:, RCH * c:RCH * (c + 1), :]).then_inc(stored, 16)
            sp.wait_ge(stored, 16 * NCH)

        @block.gpsimd
        def _(pool):
            nc.gpsimd.memset(ident[:, :], 0.0).then_inc(consts, 1)
            nc.gpsimd.memset(tri[:, :], 1.0).then_inc(consts, 1)
            nc.gpsimd.memset(onesf[:, :], 1.0).then_inc(consts, 1)
            nc.gpsimd.memset(onesb[:, :], 1.0).then_inc(consts, 1)
            nc.gpsimd.memset(h2[:, :, :, H:C], 1.0).then_inc(consts, 1)
            nc.gpsimd.iota(winrow[:, :], [[0, 1]], base=-D, channel_multiplier=1, allow_small_or_imprecise_dtypes=True).then_inc(consts, 1)
            nc.gpsimd.iota(scrapc[:, :], [[0, 1]], base=SCRAP, channel_multiplier=1, allow_small_or_imprecise_dtypes=True).then_inc(consts, 1)
            pool.wait_ge(consts, 7)
            nc.gpsimd.affine_select(out=ident[:, :], in_=ident[:, :], compare_op=ALU.not_equal, fill=1.0, base=0,
                                    pattern=[[-1, P]], channel_multiplier=1).then_inc(consts, 1)
            nc.gpsimd.affine_select(out=tri[:, :], in_=tri[:, :], compare_op=ALU.is_ge, fill=0.0, base=0,
                                    pattern=[[-1, P]], channel_multiplier=1).then_inc(consts, 1)
            pool.wait_ge(x_used, 1)
            pool.wait_ge(wz_in, 16 * 7)
            nc.gpsimd.tensor_tensor(x_sb[:, :, :], x_sb[:, :, :], bbb[:, :].unsqueeze(1).broadcast_to([P, RB, D]), ALU.add).then_inc(xbb_ready, 1)

            pool.wait_ge(mode_ready, 1)
            pool.wait_ge(table_stored, 16)
            pool.wait_ge(cols_in, 32)

            nought = pool.alloc_register("nought")
            bound = pool.alloc_register("bound")
            pool.wait_ge(zeroed, 1)
            pool.reg_load(nought, zeros[0:1, 0:1].bitcast(i32))

            def step(i, j, general):
                if general and live(i, j + 1):
                    s = (j + 1) % 2
                    n = UNROLL * i + j + 1
                    wait(pool, gathered[s], 16 * TPG * (4 * i + (j + 1) // 2))
                    wait(pool, l1_done, n - 1)
                    nc.gpsimd.tensor_copy(gidx[:, s, :], dstI[:, ds(TPG * n, TPG)]).then_inc(gidx_ready, 1)
                    pool.wait_ge(gidx_ready, n + 1)
                    pool.reg_add(bound, nought, NROWS - 1)
                    for t in range(TPG):
                        nc.gpsimd.indirect_dma_start(out=X[:, s, t, :], out_offset=None, in_=table,
                                                     in_offset=bass.IndirectOffsetOnAxis(ap=gidx[:, s, t:t + 1], axis=0), bounds_check=bound).then_inc(gathered[s], 16)
                if not live(i, j) or j < 0:
                    return
                g = UNROLL * i + j
                for t in range(TPG):
                    k = TPG * (j % 2) + t
                    if isinstance(i, int) and i == 0 and j < 2:
                        pool.wait_ge(sums_zeroed[k], 16)
                    wait(pool, added[k], 16 * (4 * i + j // 2))
                    if t == 0:
                        pool.wait_ge(idx_ready, g + 1)
                        pool.wait_ge(scat_ready, g + 1)
                    pool.reg_add(bound, nought, NROWS - 1)
                    nc.gpsimd.indirect_dma_start(out=sums[k], out_offset=bass.IndirectOffsetOnAxis(ap=idx[:, j, t:t + 1], axis=0),
                                                 in_=scat[:, j % 4, t, :], in_offset=None, bounds_check=bound,
                                                 compute_op=ALU.add).then_inc(added[k], 16)

            general = pool.value_load(mode[0:1, 0:1], min_val=0, max_val=1)
            with pool.If(general == 0):
                run_steps(pool, lambda i, j: step(i, j, False), 0, 0)
            with pool.If(general == 1):
                run_steps(pool, lambda i, j: step(i, j, True), 1, 0)

        @block.scalar
        def _(act):
            act.wait_ge(zeroed, 1)
            for k in range(NSETS):
                act.dma_start(sums[k].rearrange("(p a b) c -> p a (b c)", p=P, b=4),
                              zeros[:, 0:4 * C].unsqueeze(1).broadcast_to([P, RB // 4, 4 * C])).then_inc(sums_zeroed[k], 16)
            act.dma_start(wax[:, :], wat[0:D, :]).then_inc(wz_in, 16)
            act.dma_start(waa[:, :], wat[D:D + H, :]).then_inc(wz_in, 16)
            act.dma_start(wau[:, :], wat[D + H:D + H + DU, :]).then_inc(wz_in, 16)
            act.dma_start(wb[:, :], wbt).then_inc(wz_in, 16)
            with nc.allow_non_contiguous_dma("two columns of a float per partition"):
                act.dma_start(u0[:, :], u[0:1, :].rearrange("a k -> k a")).then_inc(wz_in, 16)
                act.dma_start(bac[:, :], ba.rearrange("(k a) -> k a", a=1)).then_inc(wz_in, 16)
            act.dma_start(bbb[:, :], bb.partition_broadcast(P)).then_inc(wz_in, 16)
            act.wait_ge(ln_centred, 1)
            nc.scalar.activation(sq, h_sb[:, :, :], ACT.Square).then_inc(ln_squared, 1)
            act.wait_ge(ln_var, 1)
            nc.scalar.activation(stat[:, 2, :], stat[:, 1, :], ACT.Sqrt, bias=epsc[:, :], scale=1.0 / D).then_inc(ln_std, 1)
            for c in range(NCH):
                act.wait_ge(hT_psum, c + 1)
                nc.scalar.activation(hT[:, c * GE:(c + 1) * GE], bank[0:D, c % 2, :], ACT.Copy).then_inc(hT_ready, 1)
            act.wait_ge(src_masked, 2)
            nc.scalar.activation(srcR[:, :, :], src_ri, ACT.Copy).then_inc(srcR_ready, 1)
            act.wait_ge(zb_psum, 1)
            nc.scalar.activation(biasz[:, :], bank[:, 6, 0:1], ACT.Identity, bias=bac[:, :]).then_inc(biasz_ready, 1)
            act.wait_ge(table_stored, 16)

            def step(i, j):
                if live(i, j):
                    g = UNROLL * i + j
                    act.wait_ge(l1_done, g + 1)
                    wait(act, l2_done, g - 1)
                    nc.scalar.activation(h1[:, j % 2, :], psL1(j % 2), ACT.Relu).then_inc(h1_ready, 1)
                if live(i, j - 1):
                    g = UNROLL * i + j - 1
                    act.wait_ge(l2_done, g + 1)
                    wait(act, sum_done, g - 1)
                    nc.scalar.activation(h2[:, (j - 1) % 2, :, 0:H], psL2((j - 1) % 2).rearrange("p (t f) -> p t f", t=TPG), ACT.Relu).then_inc(h2_ready, 1)
                if live(i, j - 2):
                    g = UNROLL * i + j - 2
                    act.wait_ge(sum_done, g + 1)
                    for t in range(TPG):
                        wait(act, added[TPG * (j % 2) + t], 16 * (4 * i + (j - 2) // 2 - 1))
                    nc.scalar.activation(scat[:, (j - 2) % 4, :, :].rearrange("p (a t) c -> p a (t c)", a=2), psSum, ACT.Copy).then_inc(scat_ready, 1)

            run_steps(act, step, 0, 2)

            for c in range(NCH + 2):
                if c < NCH:
                    act.wait_ge(aggT_psum, c + 1)
                    if c >= 2:
                        act.wait_ge(z_psum, c - 1)
                    nc.scalar.activation(aggT[:, c % 2, :], bank[:, c % 2, :], ACT.Copy).then_inc(aggT_ready, 1)
                if 1 <= c <= NCH:
                    act.wait_ge(z_psum, c)
                    if c >= 3:
                        act.wait_ge(o_psum, c - 2)
                    nc.scalar.activation(zT[:, (c - 1) % 2, :], bank[:, 2 + (c - 1) % 2, :], ACT.Relu, bias=biasz[:, :]).then_inc(z_ready, 1)

        @block.vector
        def _(dve):
            V = nc.vector
            count = [0]

            def link(ins):
                count[0] += 1
                ins.then_inc(dve_step, 1)
                dve.wait_ge(dve_step, count[0])

            V.memset(zeros[:, :], 0.0).then_inc(zeroed, 1)
            V.memset(epsc[:, :], EPS).then_inc(zeroed, 1)
            V.memset(dstR[SELP:P, :, :], 0.0)
            link(V.memset(viol[:, :], 0.0))
            dve.wait_ge(x_in, 16)
            link(V.tensor_reduce(stat[:, 0, :], x_sb[:, :, :], axis=AX.X, op=ALU.add))
            link(V.tensor_scalar(stat[:, 3, :], stat[:, 0, :], 1.0 / D, None, ALU.mult))
            V.tensor_tensor(h_sb[:, :, :], x_sb[:, :, :], stat[:, 3, :].unsqueeze(2).broadcast_to([P, RB, D]), ALU.subtract).then_inc(ln_centred, 1)
            dve.wait_ge(rows_in, 48)
            V.tensor_scalar(src_ri[0:SELP], src_ri[0:SELP], 127, None, ALU.bitwise_and).then_inc(src_masked, 1)
            V.tensor_scalar(src_ri[SELP:P], src_ri[SELP:P], 0x7fffff80, None, ALU.bitwise_and).then_inc(src_masked, 1)
            dve.wait_ge(ln_squared, 1)
            V.tensor_reduce(stat[:, 1, :], sq, axis=AX.X, op=ALU.add).then_inc(ln_var, 1)
            link(V.tensor_copy(dst0[:, :], dst_ri[0:SELP, :, 0]))
            dve.wait_ge(ln_std, 1)
            link(V.reciprocal(stat[:, 0, :], stat[:, 2, :]))
            V.scalar_tensor_tensor(out=h_sb[:, :, :], in0=h_sb[:, :, :], scalar=0.0, in1=stat[:, 0, :].unsqueeze(2).broadcast_to([P, RB, D]),
                                   op0=ALU.max, op1=ALU.mult).then_inc(h_ready, 1)
            dve.wait_ge(h_ready, 1)
            V.memset(viol[:, 5:6], 0.0).then_inc(x_used, 1)
            dve.wait_ge(w_in, 16 * 5)

            def evacuate(c):
                dve.wait_ge(p_psum, c + 1)
                V.tensor_tensor(p_sb[:, RCH * c:RCH * (c + 1), :], bank[:, 2 + c % 2, :].rearrange("p (r f) -> p r f", r=RCH),
                                b1b[:, :].unsqueeze(1).broadcast_to([P, RCH, H]), ALU.add).then_inc(p_ready, 1)

            for c in range(NCH):
                evacuate(c)
            half = (WIN - 1) / 2
            link(V.scalar_tensor_tensor(out=dst_rf[0:SELP], in0=dst_ri[0:SELP], scalar=half, in1=dst0[:, :].unsqueeze(2).broadcast_to([SELP, UNROLL, GE]),
                                        op0=ALU.subtract, op1=ALU.subtract))
            link(V.tensor_reduce(viol[0:SELP, 0:1], dst_rf[0:SELP], axis=AX.XY, op=ALU.max, apply_absolute_value=True))
            V.tensor_scalar(viol[:, 1:2], viol[:, 0:1], half + 0.5, None, ALU.is_gt).then_inc(viol_ready, 1)
            dve.wait_ge(viol_sum, 1)
            link(V.tensor_scalar(viol[:, 2:3], bank[:, 7, 0:1], 0.0, None, ALU.is_gt))
            V.tensor_copy(mode[0:1, 0:1], viol[0:1, 2:3]).then_inc(mode_ready, 1)
            link(V.tensor_scalar(viol[:, 3:4], viol[:, 2:3], -1.0, 1.0, ALU.mult, ALU.add))
            link(V.tensor_scalar(viol[:, 4:5], viol[:, 2:3], -1000.0 - half, half, ALU.mult, ALU.add))
            link(V.tensor_scalar(dstR[0:SELP], dst_rf[0:SELP], viol[0:SELP, 3:4], viol[0:SELP, 4:5], ALU.mult, ALU.add))
            dve.wait_ge(consts, 9)
            link(V.tensor_tensor(sel[:, :], ident[:, 0:SELP], ident[:, SELP:2 * SELP], ALU.add))
            dve.wait_ge(cols_in, 32)
            link(V.tensor_copy(srcF[:, :], srcI[:, :]))
            link(V.tensor_scalar(toscrap[:, :], srcF[:, :], -1.0, scrapc[:, :], ALU.mult, ALU.add))
            link(V.tensor_copy(b2p[:, 0, :], b2b[:, :]))
            link(V.tensor_tensor(b2w[:, 0, :], b2b[:, :], b2p[:, 0, :], ALU.subtract))
            link(V.tensor_copy(b2p[:, 1, :], b2w[:, 0, :]))
            link(V.tensor_tensor(b2w[:, 1, :], b2w[:, 0, :], b2p[:, 1, :], ALU.subtract))
            link(V.tensor_copy(b2p[:, 2, :], b2w[:, 1, :]))
            link(V.tensor_scalar(b2w[:, 0, :], b2p[:, 0, :], ident[:, 0:1], None, ALU.mult))
            link(V.scalar_tensor_tensor(out=b2w[:, 1, :], in0=b2p[:, 1, :], scalar=ident[:, 1:2], in1=b2w[:, 0, :], op0=ALU.mult, op1=ALU.add))
            link(V.scalar_tensor_tensor(out=b2w[:, 0, :], in0=b2p[:, 2, :], scalar=ident[:, 2:3], in1=b2w[:, 1, :], op0=ALU.mult, op1=ALU.add))
            V.tensor_copy(b2R[:, :, :], b2w[:, 0, :].unsqueeze(1).broadcast_to([P, TPG, H])).then_inc(tables_ready, 1)
            dve.wait_ge(tables_ready, 1)
            dve.wait_ge(table_stored, 16)

            def step(i, j):
                if live(i, j):
                    g = UNROLL * i + j
                    dve.wait_ge(bcast_done, g + 1)
                    wait(dve, l1_done, g - UNROLL + 1)
                    V.tensor_scalar(R[D:P, j, :], psDst[D:P, :], winrow[D:P, :], None, ALU.is_equal).then_inc(oh_ready, 1)
                    wait(dve, sum_done, g - 3)
                    for t in range(TPG):
                        mask = V.scalar_tensor_tensor(out=S[:, j % 4, t, :], in0=psSrc[:, t * TILE:(t + 1) * TILE], scalar=srcF[:, ds(TPG * g + t, 1)],
                                                      in1=tri[:, :], op0=ALU.is_equal, op1=ALU.mult, accum_out=cnt[:, j, t:t + 1])
                    mask.then_inc(mask_ready, 1)
                if live(i, j - 1):
                    g = UNROLL * i + j - 1
                    dve.wait_ge(mask_ready, g + 1)
                    wait(dve, idx_ready, g - 1)
                    V.scalar_tensor_tensor(out=extra[:, (j - 1) % 2, :], in0=cnt[:, (j - 1) % UNROLL, :], scalar=1.5, in1=toscrap[:, ds(TPG * g, TPG)],
                                           op0=ALU.is_gt, op1=ALU.mult).then_inc(extra_ready, 1)
                if live(i, j - 2):
                    g = UNROLL * i + j - 2
                    dve.wait_ge(extra_ready, g + 1)
                    wait(dve, scat_ready, g - 3)
                    V.tensor_tensor(idx[:, (j - 2) % UNROLL, :], extra[:, (j - 2) % 2, :], srcF[:, ds(TPG * g, TPG)], ALU.add).then_inc(idx_ready, 1)

            run_steps(dve, step, 0, 2)

            dve.wait_ge(xbb_ready, 1)
            for c in range(NCH + 2):
                if c < NCH:
                    s = c % 2
                    dve.wait_ge(acc_in[s], 16 * NSETS * (c // 2 + 1))
                    V.tensor_tensor(s4, SA[:, s, 0:4, :].rearrange("p k c -> p (k c)"), SA[:, s, 4:8, :].rearrange("p k c -> p (k c)"), ALU.add).then_inc(s4_done, 1)
                    dve.wait_ge(s4_done, c + 1)
                    link(V.tensor_tensor(s2, s4[:, 0:2 * KC], s4[:, 2 * KC:4 * KC], ALU.add))
                    link(V.tensor_tensor(s1, s2[:, 0:KC], s2[:, KC:2 * KC], ALU.add))
                    s1v = s1.rearrange("p (r c) -> p r c", r=RCH)
                    link(V.tensor_scalar(rc[:, 0, :], s1v[:, :, H], 1.0, None, ALU.max))
                    link(V.reciprocal(rc[:, 1, :], rc[:, 0, :]))
                    if c >= 2:
                        dve.wait_ge(aggT_psum, c - 1)
                    V.tensor_tensor(agg[:, s, :, :], s1v[:, :, 0:H], rc[:, 1, :].unsqueeze(2).broadcast_to([P, RCH, H]), ALU.mult).then_inc(agg_ready, 1)
                    dve.wait_ge(agg_ready, c + 1)
                if c >= 2:
                    n = c - 2
                    dve.wait_ge(o_psum, n + 1)
                    V.tensor_tensor(o_sb[:, RCH * n:RCH * (n + 1), :], bank[:, 4 + n % 2, 0:RCH * D].rearrange("p (r f) -> p r f", r=RCH),
                                    x_sb[:, RCH * n:RCH * (n + 1), :], ALU.add).then_inc(o_ready, 1)

        @block.tensor
        def _(pe):
            T = nc.tensor
            pe.wait_ge(consts, 9)
            pe.wait_ge(h_ready, 1)
            pe.wait_ge(w_in, 16 * 5)
            for c in range(NCH + 1):
                if c < NCH:
                    if c >= 2:
                        pe.wait_ge(hT_ready, c - 1)
                    for r in range(RCH):
                        last = T.transpose(bank[0:D, c % 2, r * P:(r + 1) * P], h_sb[:, RCH * c + r, :], ident[:, :])
                    last.then_inc(hT_psum, 1)
                if c >= 1:
                    n = c - 1
                    pe.wait_ge(hT_ready, n + 1)
                    if n >= 2:
                        pe.wait_ge(p_ready, n - 1)
                    for r in range(RCH):
                        last = T.matmul(bank[:, 2 + n % 2, r * H:(r + 1) * H], hT[:, n * GE + r * P:n * GE + (r + 1) * P], w1x[:, :], start=True, stop=True)
                    last.then_inc(p_psum, 1)
            pe.wait_ge(viol_ready, 1)
            T.matmul(bank[:, 7, 0:1], onesf[:, :], viol[:, 1:2], start=True, stop=True).then_inc(viol_sum, 1)
            pe.wait_ge(wz_in, 16 * 7)
            T.matmul(bank[:, 6, 0:1], wau[:, :], u0[:, :], start=True, stop=True).then_inc(zb_psum, 1)
            pe.wait_ge(tables_ready, 1)
            pe.wait_ge(srcR_ready, 1)
            pe.wait_ge(mode_ready, 1)
            pe.wait_ge(biasz_ready, 1)
            pe.wait_ge(p_ready, NCH)

            def step(i, j, general):
                if live(i, j) and j >= 0:
                    g = UNROLL * i + j
                    pe.wait_ge(oh_ready, g + 1)
                    pe.wait_ge(ea_in[j // 2], 16 * (i + 1))
                    pe.wait_ge(win_in[j], 16 * (i + 1))
                    wait(pe, h1_ready, g - 1)
                    if not general:
                        T.matmul(psL1(j % 2), L[:, j, :], R[:, j, :], start=True, stop=True).then_inc(l1_done, 1)
                    else:
                        T.matmul(psL1(j % 2), L[:, j, :], R[:, j, :], start=True, stop=False)
                        pe.wait_ge(gathered[j % 2], 16 * TPG * (4 * i + j // 2 + 1))
                        for t in range(TPG):
                            last = T.matmul(psL1(j % 2)[:, t * TILE:(t + 1) * TILE], X[:, j % 2, t, :], ident[:, :], start=False, stop=t == TPG - 1)
                        last.then_inc(l1_done, 1)
                if live(i, j - 1) and j - 1 >= -1:
                    g = UNROLL * i + j - 1
                    s = (j - 1) % 2
                    pe.wait_ge(h1_ready, g + 1)
                    wait(pe, h2_ready, g - 1)
                    T.matmul(psL2(s), onesb[:, :], b2R[:, :, :].rearrange("p t f -> p (t f)"), start=True, stop=False)
                    for t in range(TPG):
                        last = T.matmul(psL2(s)[:, t * H:(t + 1) * H], h1[:, s, t * TILE:(t + 1) * TILE], w2[:, :], start=False, stop=t == TPG - 1)
                    last.then_inc(l2_done, 1)
                if live(i, j - 2):
                    g = UNROLL * i + j - 2
                    pe.wait_ge(h2_ready, g + 1)
                    pe.wait_ge(mask_ready, g + 1)
                    wait(pe, scat_ready, g)
                    for t in range(TPG):
                        last = T.matmul(bank[:, 6 + t // 2, (t % 2) * C:(t % 2 + 1) * C], S[:, (j - 2) % 4, t, :], h2[:, (j - 2) % 2, t, :], start=True, stop=True)
                    last.then_inc(sum_done, 1)
                if live(i, j + 2):
                    g = UNROLL * i + j + 2
                    jj = (j + 2) % UNROLL
                    col = i + (j + 2) // UNROLL
                    one = sel[:, ds(col, 1)].broadcast_to([P, P])
                    wait(pe, oh_ready, g)
                    T.matmul(psDst, one, dstR[:, jj, :], start=True, stop=True)
                    wait(pe, mask_ready, g)
                    T.matmul(psSrc, one, srcR[:, jj, :], start=True, stop=True).then_inc(bcast_done, 1)

            general = pe.value_load(mode[0:1, 0:1], min_val=0, max_val=1)
            with pe.If(general == 0):
                run_steps(pe, lambda i, j: step(i, j, False), 2, 2)
            with pe.If(general == 1):
                run_steps(pe, lambda i, j: step(i, j, True), 2, 2)

            pe.wait_ge(scat_ready, NG)
            for c in range(NCH + 2):
                if c < NCH:
                    pe.wait_ge(agg_ready, c + 1)
                    if c >= 2:
                        pe.wait_ge(aggT_ready, c - 1)
                    for r in range(RCH):
                        last = T.transpose(bank[:, c % 2, r * P:(r + 1) * P], agg[:, c % 2, r, :], ident[:, :])
                    last.then_inc(aggT_psum, 1)
                if 1 <= c <= NCH:
                    n = c - 1
                    pe.wait_ge(aggT_ready, n + 1)
                    if n >= 2:
                        pe.wait_ge(z_ready, n - 1)
                    T.matmul(bank[:, 2 + n % 2, :], wax[:, :], hT[:, n * GE:(n + 1) * GE], start=True, stop=False)
                    T.matmul(bank[:, 2 + n % 2, :], waa[:, :], aggT[:, n % 2, :], start=False, stop=True).then_inc(z_psum, 1)
                if c >= 2:
                    n = c - 2
                    pe.wait_ge(z_ready, n + 1)
                    if n >= 2:
                        pe.wait_ge(o_ready, n - 1)
                    for r in range(RCH):
                        last = T.matmul(bank[:, 4 + n % 2, r * D:(r + 1) * D], zT[:, n % 2, r * P:(r + 1) * P], wb[:, :], start=True, stop=True)
                    last.then_inc(o_psum, 1)


def kernel(x, src, dst, edge_attr_64, L0_gnn_u, L0_gnn_W1, L0_gnn_b1, L0_gnn_W2, L0_gnn_b2, L0_gnn_Wa, L0_gnn_ba, L0_gnn_Wb, L0_gnn_bb):
    import numpy as np
    import concourse.bacc as bacc
    from concourse.bass_utils import run_bass_kernel_spmd

    def pad(a, n, fill):
        a = np.asarray(a)
        return np.concatenate([a, np.full((n - a.shape[0],) + a.shape[1:], fill, a.dtype)])

    rows = SELP * UNROLL * GE
    src_p = pad(src, rows, NROWS - 1)
    dst_p = pad(dst, rows, N - 1)
    arrays = {
        "x": pad(x, NROWS, 0),
        "src_cols": np.ascontiguousarray(src_p[:NT * TILE].reshape(NT, TILE).T),
        "dst_cols": np.ascontiguousarray(dst_p[:NT * TILE].reshape(NT, TILE).T),
        "src_rows": src_p.reshape(SELP, UNROLL, GE),
        "dst_rows": dst_p.reshape(SELP, UNROLL, GE),
        "ea": np.ascontiguousarray(pad(edge_attr_64, NG * GE, 0).reshape(NG // 2, 2 * GE, D).transpose(0, 2, 1)),
        "u": np.asarray(L0_gnn_u),
        "w1t": np.ascontiguousarray(np.asarray(L0_gnn_W1).T),
        "b1": np.asarray(L0_gnn_b1),
        "w2t": np.ascontiguousarray(np.asarray(L0_gnn_W2).T),
        "b2": np.asarray(L0_gnn_b2),
        "wat": np.ascontiguousarray(np.asarray(L0_gnn_Wa).T),
        "ba": np.asarray(L0_gnn_ba),
        "wbt": np.ascontiguousarray(np.asarray(L0_gnn_Wb).T),
        "bb": np.asarray(L0_gnn_bb),
    }
    nc = bacc.Bacc("TRN2", target_bir_lowering=False, num_devices=1)
    args = {}
    for name, a in arrays.items():
        args[name] = nc.dram_tensor(f"in_{name}", a.shape, mybir.dt.from_np(a.dtype), kind="ExternalInput").ap()
    out = nc.dram_tensor("out", (NROWS, D), mybir.dt.float32, kind="ExternalOutput").ap()
    build(nc, out=out, **args)
    r = run_bass_kernel_spmd(nc, [{f"in_{name}": a for name, a in arrays.items()}], core_ids=[0])
    return r.results[0]["out"][:N]
```

```python
import concourse.bass as bass
from concourse import mybir
from contextlib import ExitStack

N, E, D, H, DU = 6250, 206250, 64, 128, 32
P = 128
TILE = 128
TPG = 4
GE = TILE * TPG
UNROLL = 8
STEPS = -(-E // (GE * UNROLL))
NG = -(-E // GE)
NT = NG * TPG
PAIRS = -(-NG // 2)
WIN = 64
SELP = 64
RB = -(-N // (P * 4)) * 4
NROWS = P * RB
RCH = 4
NCH = RB // RCH
HALVES = [(0, 7), (7, NCH)]
C = H + 1
SCRAP = N
GRING, GLEAD = 4, 3
NACC = 4
NSETS = 4
EPS = 1e-5
assert STEPS <= SELP and N + P < NROWS and N + WIN <= NROWS


def build(nc, x, src_cols, dst_cols, src_rows, dst_rows, ea, u, w1t, b1, w2t, b2, wat, ba, wbt, bb, out):
    f32, bf16, i32 = mybir.dt.float32, mybir.dt.bfloat16, mybir.dt.int32
    ALU = mybir.AluOpType
    ACT = mybir.ActivationFunctionType
    AX = mybir.AxisListType
    ds = bass.ds

    table = nc.dram_tensor("p_table", (NROWS, H), f32, kind="Internal").ap()
    sums = nc.dram_tensor("sums", (NSETS * NROWS, C), f32, kind="Internal").ap()

    ctx = ExitStack()
    with ctx:
        def sb(name, shape, dt):
            return ctx.enter_context(nc.sbuf_tensor(name, shape, dt))

        def sem(name):
            return ctx.enter_context(nc.semaphore(name))

        x_sb = sb("x_sb", [P, RB, D], f32)
        h_sb = sb("h_sb", [P, RB, D], f32)
        o_sb = h_sb
        hT_all = sb("hT", [P, NROWS], f32)
        hT = hT_all[0:D, :]
        sq = hT_all[:, NROWS - RB * D:NROWS].rearrange("p (r f) -> p r f", f=D)
        RW = UNROLL * GE
        KC = RCH * C
        regA = sb("regA", [P, max(2 * RW, 4 * 2 * GE + 4 * TPG * C + GRING * TPG * H)], f32)
        src_ri = regA[:, 0:RW].bitcast(i32).rearrange("p (b e) -> p b e", e=GE)
        src_rf = regA[:, 0:RW].rearrange("p (b e) -> p b e", e=GE)
        dst_ri = regA[0:SELP, RW:2 * RW].bitcast(i32).rearrange("p (b e) -> p b e", e=GE)
        R = regA[:, 0:4 * 2 * GE].rearrange("p (q e) -> p q e", q=UNROLL)
        o1 = 4 * 2 * GE
        scat = regA[:, o1:o1 + 4 * TPG * C].rearrange("p (s t c) -> p s t c", s=4, c=C)
        o2 = o1 + 4 * TPG * C
        X = regA[:, o2:o2 + GRING * TPG * H].rearrange("p (s t f) -> p s t f", s=GRING, f=H)
        regB = sb("regB", [P, max(RB * H, NACC * NSETS * KC)], f32)
        p_sb = regB[:, 0:RB * H].rearrange("p (r f) -> p r f", f=H)
        SA = regB[:, 0:NACC * NSETS * KC].rearrange("p (s k c) -> p s k c", s=NACC, k=NSETS)
        srcR = sb("srcR", [P, UNROLL, GE], bf16)
        dstR = sb("dstR", [P, UNROLL, GE], bf16)
        far = hT_all[0:SELP, 0:RW // 2].bitcast(bf16)
        srcI = sb("srcI", [P, NT], i32)
        srcF = sb("srcF", [P, NT], f32)
        home = sb("home", [P, NT], f32)
        toscrap = sb("toscrap", [P, NT], f32)
        dstI = sb("dstI", [P, NT], i32)
        base = sb("base", [1, SELP * UNROLL], i32)
        L = sb("L", [P, UNROLL, H], f32)
        S = sb("S", [P, 4, TPG, TILE], f32)
        h1 = sb("h1", [P, 2, GE], f32)
        h2 = sb("h2", [P, 2, TPG, C], f32)
        cnt = sb("cnt", [P, UNROLL, TPG], f32)
        extra = sb("extra", [P, 2, TPG], f32)
        idx = sb("idx", [P, UNROLL, TPG], i32)
        gidx = sb("gidx", [P, GRING, TPG], i32)
        zeros = sb("zeros", [P, C * 10], f32)
        ident = sb("ident", [P, P], f32)
        tri = sb("tri", [P, P], f32)
        onesf = sb("onesf", [P, P], f32)
        onesb = sb("onesb", [P, P], bf16)
        sel = sb("sel", [P, SELP], bf16)
        winrow = sb("winrow", [P, 1], f32)
        oh_row = sb("oh_row", [P, 1], f32)
        scrapc = sb("scrapc", [P, 1], f32)
        epsc = sb("epsc", [P, 1], f32)
        midc = sb("midc", [P, 2], f32)
        tabrow = sb("tabrow", [P, TPG], f32)
        w1x = sb("w1x", [D, H], f32)
        w2 = sb("w2", [H, H], f32)
        wax = sb("wax", [D, H], f32)
        waa = sb("waa", [H, H], f32)
        wau = sb("wau", [DU, H], f32)
        wb = sb("wb", [H, D], f32)
        u0 = sb("u0", [DU, 1], f32)
        b1b = sb("b1b", [P, H], f32)
        b2b = sb("b2b", [P, H], f32)
        b2w = sb("b2w", [P, 2, H], f32)
        b2p = sb("b2p", [P, 3, H], bf16)
        b2R = sb("b2R", [P, TPG, H], bf16)
        bac = sb("bac", [H, 1], f32)
        biasz = sb("biasz", [H, 1], f32)
        bbb = sb("bbb", [P, D], f32)
        stat = sb("stat", [P, 5, RB], f32)
        viol = sb("viol", [P, 6], f32)
        mode = sb("mode", [1, 1], i32)
        rc = sb("rc", [P, 2, RCH], f32)

        def take(width, at=[0]):
            at[0] += width
            return regA[:, at[0] - width:at[0]]

        s2, s1 = take(2 * KC), take(KC)
        agg = take(2 * GE).rearrange("p (s r f) -> p s r f", s=2, f=H)
        aggT = take(2 * GE).rearrange("p (s e) -> p s e", s=2)
        zT = take(2 * GE).rearrange("p (s e) -> p s e", s=2)

        bank = ctx.enter_context(nc.psum_tensor("bank", [P, 8, 512], f32))
        psDst, psSrc = bank[:, 0, :], bank[:, 1, :]

        def psL1(s):
            return bank[:, 2 + s, :]

        def psL2(s):
            return bank[:, 4 + s, :]

        psSum = bank[:, 6:8, 0:2 * C]

        x_in = [sem(f"x_in{n}") for n in range(2)]
        src_rows_in = sem("src_rows_in")
        dst_rows_in = sem("dst_rows_in")
        src_cols_in = sem("src_cols_in")
        dst_cols_in = sem("dst_cols_in")
        base_in = sem("base_in")
        w1_in = sem("w1_in")
        w2_in = sem("w2_in")
        b2_in = sem("b2_in")
        wz_in = sem("wz_in")
        consts = sem("consts")
        zeroed = sem("zeroed")
        sums_zeroed = sem("sums_zeroed")
        dve_step = sem("dve_step")
        act_step = sem("act_step")
        ln_centred = sem("ln_centred")
        ln_squared = sem("ln_squared")
        ln_var = sem("ln_var")
        ln_std = sem("ln_std")
        h_ready = sem("h_ready")
        hT_psum = sem("hT_psum")
        hT_ready = sem("hT_ready")
        p_psum = sem("p_psum")
        p_ready = sem("p_ready")
        table_stored = sem("table_stored")
        far_ready = sem("far_ready")
        viol_sum = sem("viol_sum")
        mode_ready = sem("mode_ready")
        src_high = sem("src_high")
        srcR_ready = sem("srcR_ready")
        dstR_ready = sem("dstR_ready")
        srcF_ready = sem("srcF_ready")
        toscrap_ready = sem("toscrap_ready")
        home_ready = sem("home_ready")
        sel_ready = sem("sel_ready")
        b2_ready = sem("b2_ready")
        xbb_ready = sem("xbb_ready")
        zb_psum = sem("zb_psum")
        biasz_ready = sem("biasz_ready")

        ea_in = [sem(f"ea_in{q}") for q in range(4)]
        win_in = [sem(f"win_in{q}") for q in range(UNROLL)]
        bcast_done = sem("bcast_done")
        oh_ready = sem("oh_ready")
        mask_ready = sem("mask_ready")
        extra_ready = sem("extra_ready")
        idx_ready = sem("idx_ready")
        l1_done = sem("l1_done")
        h1_ready = sem("h1_ready")
        l2_done = sem("l2_done")
        h2_ready = sem("h2_ready")
        sum_done = sem("sum_done")
        scat_ready = sem("scat_ready")
        added = [sem(f"added{k}") for k in range(NSETS)]
        gidx_ready = sem("gidx_ready")
        gathered = [sem(f"gathered{s}") for s in range(GRING)]

        acc_in = [sem(f"acc_in{s}") for s in range(NACC)]
        s2_done = sem("s2_done")
        agg_ready = sem("agg_ready")
        aggT_psum = sem("aggT_psum")
        aggT_ready = sem("aggT_ready")
        z_psum = sem("z_psum")
        z_ready = sem("z_ready")
        o_psum = sem("o_psum")
        o_ready = sem("o_ready")
        stored = sem("stored")

        block = ctx.enter_context(nc.Block())

        def live(i, j):
            return not isinstance(i, int) or 0 <= UNROLL * i + j < NG

        def wait(eng, s, value):
            if not isinstance(value, int) or value > 0:
                eng.wait_ge(s, value)

        def run_steps(eng, step, lead, lag):
            for j in range(-lead, UNROLL):
                step(0, j)
            with eng.Fori(1, STEPS - 1) as i:
                for j in range(UNROLL):
                    step(i, j)
            for j in range(UNROLL + lag):
                step(STEPS - 1, j)

        @block.sync
        def _(sp):
            x_v = x.rearrange("(p r) f -> p r f", p=P)
            for n, (c0, c1) in enumerate(HALVES):
                sp.dma_start(x_sb[:, RCH * c0:RCH * c1, :], x_v[:, RCH * c0:RCH * c1, :]).then_inc(x_in[n], 16)
            sp.dma_start(dst_ri, dst_rows).then_inc(dst_rows_in, 16)
            sp.dma_start(src_ri[0:SELP, :, :], src_rows).then_inc(src_rows_in, 16)
            sp.dma_start(src_ri[SELP:P, :, :], src_rows).then_inc(src_rows_in, 16)
            sp.dma_start(w1x[:, :], w1t[0:D, :]).then_inc(w1_in, 16)
            sp.dma_start(b1b[:, :], b1.partition_broadcast(P)).then_inc(w1_in, 16)
            sp.dma_start(L[0:D, :, :], w1t[D:2 * D, :].unsqueeze(1).broadcast_to([D, UNROLL, H])).then_inc(w2_in, 16)
            sp.dma_start(w2[:, :], w2t).then_inc(w2_in, 16)
            with nc.allow_non_contiguous_dma("first dst of each group"):
                sp.dma_start(base[0:1, :], dst_rows[:, :, 0:1].rearrange("(a s) b o -> a (s b o)", a=1)).then_inc(base_in, 16)
            table_v = table.rearrange("(p r) f -> p r f", p=P)
            for c0, c1 in HALVES:
                sp.wait_ge(p_ready, c1)
                sp.dma_start(table_v[:, RCH * c0:RCH * c1, :], p_sb[:, RCH * c0:RCH * c1, :]).then_inc(table_stored, 16)
            sp.wait_ge(srcR_ready, 1)
            sp.wait_ge(dstR_ready, 1)
            sp.wait_ge(base_in, 16)
            sp.wait_ge(w2_in, 32)

            def step(i, j):
                if not live(i, j):
                    return
                g = UNROLL * i + j
                if j % 2 == 0:
                    wait(sp, l1_done, g - UNROLL + 2)
                    sp.dma_start(R[0:D, j:j + 2, :], ea[ds(4 * i + j // 2, 1)].rearrange("o f (q e) -> (o f) q e", q=2)).then_inc(ea_in[j // 2], 16)
                wait(sp, l1_done, g - UNROLL + 1)
                wait(sp, table_stored, 32)
                row = sp.value_load(base[0:1, ds(g, 1)], min_val=0, max_val=N - 1)
                sp.dma_start(L[D:P, j, :], table[ds(row, WIN), :]).then_inc(win_in[j], 16)

            run_steps(sp, step, 0, 0)

            for k in range(NSETS):
                sp.wait_ge(added[k], 16 * -(-(NT - k) // NSETS))
            sums_v = sums.rearrange("(k p r) c -> p k (r c)", k=NSETS, p=P)
            for c in range(NCH):
                wait(sp, s2_done, c - NACC + 1)
                sp.dma_start(SA[:, c % NACC, :, :], sums_v[:, :, c * KC:(c + 1) * KC]).then_inc(acc_in[c % NACC], 16)
            out_v = out.rearrange("(p r) f -> p r f", p=P)
            for c in range(NCH):
                sp.wait_ge(o_ready, c + 1)
                sp.dma_start(out_v[:, RCH * c:RCH * (c + 1), :], o_sb[:, RCH * c:RCH * (c + 1), :]).then_inc(stored, 16)
            sp.wait_ge(stored, 16 * NCH)

        @block.gpsimd
        def _(pool):
            nc.gpsimd.memset(ident[:, :], 0.0).then_inc(consts, 1)
            nc.gpsimd.memset(tri[:, :], 1.0).then_inc(consts, 1)
            nc.gpsimd.memset(onesf[:, :], 1.0).then_inc(consts, 1)
            nc.gpsimd.memset(onesb[:, :], 1.0).then_inc(consts, 1)
            nc.gpsimd.memset(h2[:, :, :, H:C], 1.0).then_inc(consts, 1)
            nc.gpsimd.iota(winrow[:, :], [[0, 1]], base=-D, channel_multiplier=1, allow_small_or_imprecise_dtypes=True).then_inc(consts, 1)
            nc.gpsimd.iota(scrapc[:, :], [[0, 1]], base=SCRAP, channel_multiplier=1, allow_small_or_imprecise_dtypes=True).then_inc(consts, 1)
            nc.gpsimd.iota(tabrow[:, :], [[NROWS, TPG]], base=0, channel_multiplier=0, allow_small_or_imprecise_dtypes=True).then_inc(consts, 1)
            pool.wait_ge(consts, 8)
            nc.gpsimd.affine_select(out=ident[:, :], in_=ident[:, :], compare_op=ALU.not_equal, fill=1.0, base=0,
                                    pattern=[[-1, P]], channel_multiplier=1).then_inc(consts, 1)
            nc.gpsimd.affine_select(out=tri[:, :], in_=tri[:, :], compare_op=ALU.is_ge, fill=0.0, base=0,
                                    pattern=[[-1, P]], channel_multiplier=1).then_inc(consts, 1)
            pool.wait_ge(src_high, 2)
            pool.wait_ge(consts, 10)
            nc.gpsimd.tensor_tensor(srcR[SELP:P], src_rf[SELP:P], srcR[SELP:P], ALU.subtract).then_inc(srcR_ready, 1)
            pool.wait_ge(srcF_ready, 1)
            pool.wait_ge(srcR_ready, 1)
            nc.gpsimd.tensor_tensor(home[:, :].rearrange("p (g t) -> p g t", t=TPG), srcF[:, :].rearrange("p (g t) -> p g t", t=TPG),
                                    tabrow[:, :].unsqueeze(1).broadcast_to([P, NG, TPG]), ALU.add).then_inc(home_ready, 1)
            pool.wait_ge(ln_centred, 2)
            pool.wait_ge(wz_in, 16 * 7)
            nc.gpsimd.tensor_tensor(x_sb[:, :, :], x_sb[:, :, :], bbb[:, :].unsqueeze(1).broadcast_to([P, RB, D]), ALU.add).then_inc(xbb_ready, 1)

            pool.wait_ge(mode_ready, 1)
            pool.wait_ge(table_stored, 32)
            pool.wait_ge(dst_cols_in, 16)
            pool.wait_ge(sums_zeroed, 16 * NSETS)

            nought = pool.alloc_register("nought")
            bound = pool.alloc_register("bound")
            pool.wait_ge(zeroed, 1)
            pool.reg_load(nought, zeros[0:1, 0:1].bitcast(i32))

            def step(i, j, general):
                if general and live(i, j + GLEAD):
                    s = (j + GLEAD) % GRING
                    n = UNROLL * i + j + GLEAD
                    wait(pool, gathered[s], 16 * TPG * (UNROLL // GRING * i + (j + GLEAD) // GRING))
                    wait(pool, l1_done, n - GRING + 1)
                    nc.gpsimd.tensor_copy(gidx[:, s, :], dstI[:, ds(TPG * n, TPG)]).then_inc(gidx_ready, 1)
                    pool.wait_ge(gidx_ready, n + 1)
                    pool.reg_add(bound, nought, NROWS - 1)
                    for t in range(TPG):
                        nc.gpsimd.indirect_dma_start(out=X[:, s, t, :], out_offset=None, in_=table,
                                                     in_offset=bass.IndirectOffsetOnAxis(ap=gidx[:, s, t:t + 1], axis=0), bounds_check=bound).then_inc(gathered[s], 16)
                if not live(i, j) or j < 0:
                    return
                g = UNROLL * i + j
                for t in range(TPG):
                    k = (TPG * j + t) % NSETS
                    wait(pool, added[k], 16 * (UNROLL * TPG // NSETS * i + (TPG * j + t) // NSETS))
                    if t == 0:
                        pool.wait_ge(idx_ready, g + 1)
                        pool.wait_ge(scat_ready, g + 1)
                    pool.reg_add(bound, nought, NSETS * NROWS - 1)
                    nc.gpsimd.indirect_dma_start(out=sums, out_offset=bass.IndirectOffsetOnAxis(ap=idx[:, j, t:t + 1], axis=0),
                                                 in_=scat[:, j % 4, t, :], in_offset=None, bounds_check=bound,
                                                 compute_op=ALU.add).then_inc(added[k], 16)

            general = pool.value_load(mode[0:1, 0:1], min_val=0, max_val=1)
            with pool.If(general == 0):
                run_steps(pool, lambda i, j: step(i, j, False), 0, 0)
            with pool.If(general == 1):
                run_steps(pool, lambda i, j: step(i, j, True), GLEAD, 0)

        @block.scalar
        def _(act):
            act.dma_start(b2b[:, :], b2.partition_broadcast(P)).then_inc(b2_in, 16)
            act.dma_start(srcI[:, :], src_cols).then_inc(src_cols_in, 16)
            act.dma_start(wax[:, :], wat[0:D, :]).then_inc(wz_in, 16)
            act.dma_start(waa[:, :], wat[D:D + H, :]).then_inc(wz_in, 16)
            act.dma_start(wau[:, :], wat[D + H:D + H + DU, :]).then_inc(wz_in, 16)
            act.dma_start(wb[:, :], wbt).then_inc(wz_in, 16)
            with nc.allow_non_contiguous_dma("two columns of a float per partition"):
                act.dma_start(u0[:, :], u[0:1, :].rearrange("a k -> k a")).then_inc(wz_in, 16)
                act.dma_start(bac[:, :], ba.rearrange("(k a) -> k a", a=1)).then_inc(wz_in, 16)
            act.dma_start(bbb[:, :], bb.partition_broadcast(P)).then_inc(wz_in, 16)
            act.wait_ge(ln_centred, 1)
            (a0, a1), (a2, a3) = [(RCH * c0, RCH * c1) for c0, c1 in HALVES]
            nc.scalar.activation(sq[:, a0:a1, :], h_sb[:, a0:a1, :], ACT.Square).then_inc(ln_squared, 1)
            act.wait_ge(ln_centred, 2)
            nc.scalar.activation(sq[:, a2:a3, :], h_sb[:, a2:a3, :], ACT.Square).then_inc(ln_squared, 1)
            act.wait_ge(src_rows_in, 32)
            nc.scalar.activation(srcR[:, :, :], src_ri, ACT.Copy).then_inc(src_high, 1)
            act.wait_ge(src_high, 1)
            nc.scalar.activation(src_rf[SELP:P], src_ri[SELP:P], ACT.Copy).then_inc(src_high, 1)
            act.wait_ge(ln_var, 1)
            nc.scalar.activation(stat[:, 2, a0:a1], stat[:, 1, a0:a1], ACT.Sqrt, bias=epsc[:, :], scale=1.0 / D).then_inc(ln_std, 1)
            act.wait_ge(ln_var, 2)
            nc.scalar.activation(stat[:, 2, a2:a3], stat[:, 1, a2:a3], ACT.Sqrt, bias=epsc[:, :], scale=1.0 / D).then_inc(ln_std, 1)
            act.wait_ge(dstR_ready, 1)
            act.wait_ge(zeroed, 4)
            nc.scalar.activation(far, dstR[0:SELP].rearrange("p b e -> p (b e)"), ACT.Abs, bias=midc[0:SELP, 0:1]).then_inc(act_step, 1)
            act.wait_ge(act_step, 1)
            nc.scalar.activation(far, far, ACT.Relu, bias=midc[0:SELP, 1:2], accum_out=viol[0:SELP, 1:2]).then_inc(far_ready, 1)
            act.wait_ge(far_ready, 1)
            for c in range(NCH):
                act.wait_ge(hT_psum, c + 1)
                nc.scalar.activation(hT[:, c * GE:(c + 1) * GE], bank[0:D, c % 2, :], ACT.Copy).then_inc(hT_ready, 1)
            act.wait_ge(zeroed, 4)
            act.dma_start(dstI[:, :], dst_cols).then_inc(dst_cols_in, 16)
            for k in range(NSETS):
                act.dma_start(sums[k * NROWS:(k + 1) * NROWS, :].rearrange("(p a b) c -> p a (b c)", p=P, b=4),
                              zeros[:, 0:4 * C].unsqueeze(1).broadcast_to([P, RB // 4, 4 * C])).then_inc(sums_zeroed, 16)
            act.wait_ge(src_cols_in, 16)
            nc.scalar.activation(srcF[:, :], srcI[:, :], ACT.Copy).then_inc(srcF_ready, 1)
            act.wait_ge(srcF_ready, 1)
            act.wait_ge(consts, 10)
            nc.scalar.activation(toscrap[:, :], srcF[:, :], ACT.Identity, bias=scrapc[:, :], scale=-1.0).then_inc(toscrap_ready, 1)
            act.wait_ge(zb_psum, 1)
            nc.scalar.activation(biasz[:, :], bank[:, 6, 0:1], ACT.Identity, bias=bac[:, :]).then_inc(biasz_ready, 1)

            def step(i, j):
                if live(i, j):
                    g = UNROLL * i + j
                    act.wait_ge(l1_done, g + 1)
                    wait(act, l2_done, g - 1)
                    nc.scalar.activation(h1[:, j % 2, :], psL1(j % 2), ACT.Relu).then_inc(h1_ready, 1)
                if live(i, j - 1):
                    g = UNROLL * i + j - 1
                    act.wait_ge(l2_done, g + 1)
                    wait(act, sum_done, g - 1)
                    nc.scalar.activation(h2[:, (j - 1) % 2, :, 0:H], psL2((j - 1) % 2).rearrange("p (t f) -> p t f", t=TPG), ACT.Relu).then_inc(h2_ready, 1)
                if live(i, j - 2):
                    g = UNROLL * i + j - 2
                    act.wait_ge(sum_done, g + 1)
                    for t in range(TPG):
                        n = TPG * (j - 2 - 4) + t
                        wait(act, added[n % NSETS], 16 * (UNROLL * TPG // NSETS * i + n // NSETS + 1))
                    nc.scalar.activation(scat[:, (j - 2) % 4, :, :].rearrange("p (a t) c -> p a (t c)", a=2), psSum, ACT.Copy).then_inc(scat_ready, 1)

            run_steps(act, step, 0, 2)

            for c in range(NCH + 2):
                if c < NCH:
                    act.wait_ge(aggT_psum, c + 1)
                    if c >= 2:
                        act.wait_ge(z_psum, c - 1)
                    nc.scalar.activation(aggT[:, c % 2, :], bank[:, c % 2, :], ACT.Copy).then_inc(aggT_ready, 1)
                if 1 <= c <= NCH:
                    act.wait_ge(z_psum, c)
                    if c >= 3:
                        act.wait_ge(o_psum, c - 2)
                    nc.scalar.activation(zT[:, (c - 1) % 2, :], bank[:, 2 + (c - 1) % 2, :], ACT.Relu, bias=biasz[:, :]).then_inc(z_ready, 1)

        @block.vector
        def _(dve):
            V = nc.vector
            count = [0]

            def link(ins):
                count[0] += 1
                ins.then_inc(dve_step, 1)
                dve.wait_ge(dve_step, count[0])

            half = (WIN - 1) / 2
            V.memset(zeros[:, :], 0.0).then_inc(zeroed, 1)
            V.memset(epsc[:, :], EPS).then_inc(zeroed, 1)
            V.memset(midc[:, 0:1], -half)
            V.memset(midc[:, 1:2], -half - 0.5).then_inc(zeroed, 1)
            V.memset(dstR[SELP:P, :, :], 0.0)
            V.memset(viol[:, :], 0.0).then_inc(zeroed, 1)

            for n, (c0, c1) in enumerate(HALVES):
                r0, r1 = RCH * c0, RCH * c1
                dve.wait_ge(x_in[n], 16)
                link(V.tensor_reduce(stat[:, 0, r0:r1], x_sb[:, r0:r1, :], axis=AX.X, op=ALU.add))
                link(V.tensor_scalar(stat[:, 3, r0:r1], stat[:, 0, r0:r1], 1.0 / D, None, ALU.mult))
                V.tensor_tensor(h_sb[:, r0:r1, :], x_sb[:, r0:r1, :], stat[:, 3, r0:r1].unsqueeze(2).broadcast_to([P, r1 - r0, D]), ALU.subtract).then_inc(ln_centred, 1)
            for n, (c0, c1) in enumerate(HALVES):
                r0, r1 = RCH * c0, RCH * c1
                dve.wait_ge(ln_squared, n + 1)
                V.tensor_reduce(stat[:, 1, r0:r1], sq[:, r0:r1, :], axis=AX.X, op=ALU.add).then_inc(ln_var, 1)
            dve.wait_ge(dst_rows_in, 16)
            V.tensor_tensor(dstR[0:SELP], dst_ri, dst_ri[:, :, 0:1].broadcast_to([SELP, UNROLL, GE]), ALU.subtract).then_inc(dstR_ready, 1)
            dve.wait_ge(consts, 10)
            dve.wait_ge(b2_in, 16)
            V.tensor_tensor(sel[:, :], ident[:, 0:SELP], ident[:, SELP:2 * SELP], ALU.add).then_inc(sel_ready, 1)
            link(V.tensor_copy(b2p[:, 0, :], b2b[:, :]))
            link(V.tensor_tensor(b2w[:, 0, :], b2b[:, :], b2p[:, 0, :], ALU.subtract))
            link(V.tensor_copy(b2p[:, 1, :], b2w[:, 0, :]))
            link(V.tensor_tensor(b2w[:, 1, :], b2w[:, 0, :], b2p[:, 1, :], ALU.subtract))
            link(V.tensor_copy(b2p[:, 2, :], b2w[:, 1, :]))
            link(V.tensor_scalar(b2w[:, 0, :], b2p[:, 0, :], ident[:, 0:1], None, ALU.mult))
            link(V.scalar_tensor_tensor(out=b2w[:, 1, :], in0=b2p[:, 1, :], scalar=ident[:, 1:2], in1=b2w[:, 0, :], op0=ALU.mult, op1=ALU.add))
            link(V.scalar_tensor_tensor(out=b2w[:, 0, :], in0=b2p[:, 2, :], scalar=ident[:, 2:3], in1=b2w[:, 1, :], op0=ALU.mult, op1=ALU.add))
            V.tensor_copy(b2R[:, :, :], b2w[:, 0, :].unsqueeze(1).broadcast_to([P, TPG, H])).then_inc(b2_ready, 1)
            for n, (c0, c1) in enumerate(HALVES):
                r0, r1 = RCH * c0, RCH * c1
                dve.wait_ge(ln_std, n + 1)
                link(V.reciprocal(stat[:, 4, r0:r1], stat[:, 2, r0:r1]))
                V.scalar_tensor_tensor(out=h_sb[:, r0:r1, :], in0=h_sb[:, r0:r1, :], scalar=0.0, in1=stat[:, 4, r0:r1].unsqueeze(2).broadcast_to([P, r1 - r0, D]),
                                       op0=ALU.max, op1=ALU.mult).then_inc(h_ready, 1)
            dve.wait_ge(viol_sum, 1)
            link(V.tensor_scalar(viol[:, 2:3], bank[:, 7, 0:1], 0.0, None, ALU.is_gt))
            V.tensor_copy(mode[0:1, 0:1], viol[0:1, 2:3]).then_inc(mode_ready, 1)
            link(V.scalar_tensor_tensor(out=oh_row[:, :], in0=viol[:, 2:3], scalar=-1e6, in1=winrow[:, :], op0=ALU.mult, op1=ALU.add))
            dve.wait_ge(w1_in, 32)
            for c in range(NCH):
                dve.wait_ge(p_psum, c + 1)
                V.tensor_tensor(p_sb[:, RCH * c:RCH * (c + 1), :], bank[:, 2 + c % 2, :].rearrange("p (r f) -> p r f", r=RCH),
                                b1b[:, :].unsqueeze(1).broadcast_to([P, RCH, H]), ALU.add).then_inc(p_ready, 1)
            dve.wait_ge(srcF_ready, 1)
            dve.wait_ge(toscrap_ready, 1)
            dve.wait_ge(home_ready, 1)

            def step(i, j):
                if live(i, j):
                    g = UNROLL * i + j
                    dve.wait_ge(bcast_done, g + 1)
                    wait(dve, l1_done, g - UNROLL + 1)
                    V.tensor_scalar(R[D:P, j, :], psDst[D:P, :], oh_row[D:P, :], None, ALU.is_equal).then_inc(oh_ready, 1)
                    wait(dve, sum_done, g - 3)
                    for t in range(TPG):
                        mask = V.scalar_tensor_tensor(out=S[:, j % 4, t, :], in0=psSrc[:, t * TILE:(t + 1) * TILE], scalar=srcF[:, ds(TPG * g + t, 1)],
                                                      in1=tri[:, :], op0=ALU.is_equal, op1=ALU.mult, accum_out=cnt[:, j, t:t + 1])
                    mask.then_inc(mask_ready, 1)
                if live(i, j - 1):
                    g = UNROLL * i + j - 1
                    dve.wait_ge(mask_ready, g + 1)
                    wait(dve, idx_ready, g - 1)
                    V.scalar_tensor_tensor(out=extra[:, (j - 1) % 2, :], in0=cnt[:, (j - 1) % UNROLL, :], scalar=1.5, in1=toscrap[:, ds(TPG * g, TPG)],
                                           op0=ALU.is_gt, op1=ALU.mult).then_inc(extra_ready, 1)
                if live(i, j - 2):
                    g = UNROLL * i + j - 2
                    dve.wait_ge(extra_ready, g + 1)
                    wait(dve, scat_ready, g - 3)
                    V.tensor_tensor(idx[:, (j - 2) % UNROLL, :], extra[:, (j - 2) % 2, :], home[:, ds(TPG * g, TPG)], ALU.add).then_inc(idx_ready, 1)

            run_steps(dve, step, 0, 2)

            dve.wait_ge(xbb_ready, 1)
            for c in range(NCH + 2):
                if c < NCH:
                    s = c % NACC
                    dve.wait_ge(acc_in[s], 16 * (c // NACC + 1))
                    V.tensor_tensor(s2, SA[:, s, 0:2, :].rearrange("p k c -> p (k c)"), SA[:, s, 2:4, :].rearrange("p k c -> p (k c)"), ALU.add).then_inc(s2_done, 1)
                    dve.wait_ge(s2_done, c + 1)
                    link(V.tensor_tensor(s1, s2[:, 0:KC], s2[:, KC:2 * KC], ALU.add))
                    s1v = s1.rearrange("p (r c) -> p r c", r=RCH)
                    link(V.tensor_scalar(rc[:, 0, :], s1v[:, :, H], 1.0, None, ALU.max))
                    link(V.reciprocal(rc[:, 1, :], rc[:, 0, :]))
                    if c >= 2:
                        dve.wait_ge(aggT_psum, c - 1)
                    V.tensor_tensor(agg[:, c % 2, :, :], s1v[:, :, 0:H], rc[:, 1, :].unsqueeze(2).broadcast_to([P, RCH, H]), ALU.mult).then_inc(agg_ready, 1)
                    dve.wait_ge(agg_ready, c + 1)
                if c >= 2:
                    n = c - 2
                    dve.wait_ge(o_psum, n + 1)
                    V.tensor_tensor(o_sb[:, RCH * n:RCH * (n + 1), :], bank[:, 4 + n % 2, 0:RCH * D].rearrange("p (r f) -> p r f", r=RCH),
                                    x_sb[:, RCH * n:RCH * (n + 1), :], ALU.add).then_inc(o_ready, 1)

        @block.tensor
        def _(pe):
            T = nc.tensor
            pe.wait_ge(consts, 10)
            pe.wait_ge(w1_in, 32)
            pe.wait_ge(far_ready, 1)
            T.matmul(bank[:, 7, 0:1], onesf[:, :], viol[:, 1:2], start=True, stop=True).then_inc(viol_sum, 1)
            for c in range(NCH + 1):
                if c < NCH:
                    for n, (c0, _) in enumerate(HALVES):
                        if c == c0:
                            pe.wait_ge(h_ready, n + 1)
                    if c >= 2:
                        pe.wait_ge(hT_ready, c - 1)
                    for r in range(RCH):
                        last = T.transpose(bank[0:D, c % 2, r * P:(r + 1) * P], h_sb[:, RCH * c + r, :], ident[:, :])
                    last.then_inc(hT_psum, 1)
                if c >= 1:
                    n = c - 1
                    pe.wait_ge(hT_ready, n + 1)
                    if n >= 2:
                        pe.wait_ge(p_ready, n - 1)
                    for r in range(RCH):
                        last = T.matmul(bank[:, 2 + n % 2, r * H:(r + 1) * H], hT[:, n * GE + r * P:n * GE + (r + 1) * P], w1x[:, :], start=True, stop=True)
                    last.then_inc(p_psum, 1)
            pe.wait_ge(wz_in, 16 * 7)
            T.matmul(bank[:, 6, 0:1], wau[:, :], u0[:, :], start=True, stop=True).then_inc(zb_psum, 1)
            pe.wait_ge(sel_ready, 1)
            pe.wait_ge(b2_ready, 1)
            pe.wait_ge(srcR_ready, 1)
            pe.wait_ge(dstR_ready, 1)
            pe.wait_ge(w2_in, 32)
            pe.wait_ge(mode_ready, 1)
            pe.wait_ge(biasz_ready, 1)
            pe.wait_ge(p_ready, NCH)

            def step(i, j, general):
                if live(i, j) and j >= 0:
                    g = UNROLL * i + j
                    pe.wait_ge(oh_ready, g + 1)
                    pe.wait_ge(ea_in[j // 2], 16 * (i + 1))
                    pe.wait_ge(win_in[j], 16 * (i + 1))
                    wait(pe, h1_ready, g - 1)
                    if not general:
                        T.matmul(psL1(j % 2), L[:, j, :], R[:, j, :], start=True, stop=True).then_inc(l1_done, 1)
                    else:
                        T.matmul(psL1(j % 2), L[:, j, :], R[:, j, :], start=True, stop=False)
                        pe.wait_ge(gathered[j % GRING], 16 * TPG * (UNROLL // GRING * i + j // GRING + 1))
                        for t in range(TPG):
                            last = T.matmul(psL1(j % 2)[:, t * TILE:(t + 1) * TILE], X[:, j % GRING, t, :], ident[:, :], start=False, stop=t == TPG - 1)
                        last.then_inc(l1_done, 1)
                if live(i, j - 1) and j - 1 >= -1:
                    g = UNROLL * i + j - 1
                    s = (j - 1) % 2
                    pe.wait_ge(h1_ready, g + 1)
                    wait(pe, h2_ready, g - 1)
                    T.matmul(psL2(s), onesb[:, :], b2R[:, :, :].rearrange("p t f -> p (t f)"), start=True, stop=False)
                    for t in range(TPG):
                        last = T.matmul(psL2(s)[:, t * H:(t + 1) * H], h1[:, s, t * TILE:(t + 1) * TILE], w2[:, :], start=False, stop=t == TPG - 1)
                    last.then_inc(l2_done, 1)
                if live(i, j - 2):
                    g = UNROLL * i + j - 2
                    pe.wait_ge(h2_ready, g + 1)
                    pe.wait_ge(mask_ready, g + 1)
                    wait(pe, scat_ready, g)
                    for t in range(TPG):
                        last = T.matmul(bank[:, 6 + t // 2, (t % 2) * C:(t % 2 + 1) * C], S[:, (j - 2) % 4, t, :], h2[:, (j - 2) % 2, t, :], start=True, stop=True)
                    last.then_inc(sum_done, 1)
                if live(i, j + 2):
                    g = UNROLL * i + j + 2
                    jj = (j + 2) % UNROLL
                    col = i + (j + 2) // UNROLL
                    one = sel[:, ds(col, 1)].broadcast_to([P, P])
                    wait(pe, oh_ready, g)
                    T.matmul(psDst, one, dstR[:, jj, :], start=True, stop=True)
                    wait(pe, mask_ready, g)
                    T.matmul(psSrc, one, srcR[:, jj, :], start=True, stop=True).then_inc(bcast_done, 1)

            general = pe.value_load(mode[0:1, 0:1], min_val=0, max_val=1)
            with pe.If(general == 0):
                run_steps(pe, lambda i, j: step(i, j, False), 2, 2)
            with pe.If(general == 1):
                run_steps(pe, lambda i, j: step(i, j, True), 2, 2)

            pe.wait_ge(scat_ready, NG)
            for c in range(NCH + 2):
                if c < NCH:
                    pe.wait_ge(agg_ready, c + 1)
                    if c >= 2:
                        pe.wait_ge(aggT_ready, c - 1)
                    for r in range(RCH):
                        last = T.transpose(bank[:, c % 2, r * P:(r + 1) * P], agg[:, c % 2, r, :], ident[:, :])
                    last.then_inc(aggT_psum, 1)
                if 1 <= c <= NCH:
                    n = c - 1
                    pe.wait_ge(aggT_ready, n + 1)
                    if n >= 2:
                        pe.wait_ge(z_ready, n - 1)
                    T.matmul(bank[:, 2 + n % 2, :], wax[:, :], hT[:, n * GE:(n + 1) * GE], start=True, stop=False)
                    T.matmul(bank[:, 2 + n % 2, :], waa[:, :], aggT[:, n % 2, :], start=False, stop=True).then_inc(z_psum, 1)
                if c >= 2:
                    n = c - 2
                    pe.wait_ge(z_ready, n + 1)
                    if n >= 2:
                        pe.wait_ge(o_ready, n - 1)
                    for r in range(RCH):
                        last = T.matmul(bank[:, 4 + n % 2, r * D:(r + 1) * D], zT[:, n % 2, r * P:(r + 1) * P], wb[:, :], start=True, stop=True)
                    last.then_inc(o_psum, 1)


def kernel(x, src, dst, edge_attr_64, L0_gnn_u, L0_gnn_W1, L0_gnn_b1, L0_gnn_W2, L0_gnn_b2, L0_gnn_Wa, L0_gnn_ba, L0_gnn_Wb, L0_gnn_bb):
    import numpy as np
    import concourse.bacc as bacc
    from concourse.bass_utils import run_bass_kernel_spmd

    def pad(a, n, fill):
        a = np.asarray(a)
        return np.concatenate([a, np.full((n - a.shape[0],) + a.shape[1:], fill, a.dtype)])

    rows = SELP * UNROLL * GE
    src_p = pad(src, rows, NROWS - 1)
    dst_p = pad(dst, rows, N - 1)
    arrays = {
        "x": pad(x, NROWS, 0),
        "src_cols": np.ascontiguousarray(src_p[:NT * TILE].reshape(NT, TILE).T),
        "dst_cols": np.ascontiguousarray(dst_p[:NT * TILE].reshape(NT, TILE).T),
        "src_rows": src_p.reshape(SELP, UNROLL, GE),
        "dst_rows": dst_p.reshape(SELP, UNROLL, GE),
        "ea": np.ascontiguousarray(pad(edge_attr_64, PAIRS * 2 * GE, 0).reshape(PAIRS, 2 * GE, D).transpose(0, 2, 1)),
        "u": np.asarray(L0_gnn_u),
        "w1t": np.ascontiguousarray(np.asarray(L0_gnn_W1).T),
        "b1": np.asarray(L0_gnn_b1),
        "w2t": np.ascontiguousarray(np.asarray(L0_gnn_W2).T),
        "b2": np.asarray(L0_gnn_b2),
        "wat": np.ascontiguousarray(np.asarray(L0_gnn_Wa).T),
        "ba": np.asarray(L0_gnn_ba),
        "wbt": np.ascontiguousarray(np.asarray(L0_gnn_Wb).T),
        "bb": np.asarray(L0_gnn_bb),
    }
    nc = bacc.Bacc("TRN2", target_bir_lowering=False, num_devices=1)
    args = {}
    for name, a in arrays.items():
        args[name] = nc.dram_tensor(f"in_{name}", a.shape, mybir.dt.from_np(a.dtype), kind="ExternalInput").ap()
    out = nc.dram_tensor("out", (NROWS, D), mybir.dt.float32, kind="ExternalOutput").ap()
    build(nc, out=out, **args)
    r = run_bass_kernel_spmd(nc, [{f"in_{name}": a for name, a in arrays.items()}], core_ids=[0])
    return r.results[0]["out"][:N]
```

```python
import concourse.bass as bass
from concourse import mybir
from contextlib import ExitStack

N, E, D, H, DU = 6250, 206250, 64, 128, 32
P = 128
TILE = 128
TPG = 4
GE = TILE * TPG
UNROLL = 8
STEPS = -(-E // (GE * UNROLL))
NG = -(-E // GE)
NT = NG * TPG
PAIRS = -(-NG // 2)
WIN = 64
GPP = 4
RB = -(-N // (P * 4)) * 4
NROWS = P * RB
RCH = 4
NCH = RB // RCH
HALVES = [(0, 7), (7, NCH)]
C = H + 1
SCRAP = N
GRING, GLEAD = 4, 3
NACC = 4
OLAG = 8
NSETS = 4
EPS = 1e-5
assert NG <= P * GPP and N + P < NROWS and N + WIN <= NROWS


def build(nc, x, src_cols, dst_cols, src_rows, dst_rows, ea, u, w1t, b1, w2t, b2, wat, ba, wbt, bb, out):
    f32, bf16, i32 = mybir.dt.float32, mybir.dt.bfloat16, mybir.dt.int32
    ALU = mybir.AluOpType
    ACT = mybir.ActivationFunctionType
    AX = mybir.AxisListType
    ds = bass.ds

    table = nc.dram_tensor("p_table", (NROWS, H), f32, kind="Internal").ap()
    sums = nc.dram_tensor("sums", (NSETS * NROWS, C), f32, kind="Internal").ap()

    ctx = ExitStack()
    with ctx:
        def sb(name, shape, dt):
            return ctx.enter_context(nc.sbuf_tensor(name, shape, dt))

        def sem(name):
            return ctx.enter_context(nc.semaphore(name))

        x_sb = sb("x_sb", [P, RB, D], f32)
        h_sb = sb("h_sb", [P, RB, D], f32)
        o_sb = h_sb
        hT = sb("hT", [P, NCH, RCH // 2, P], f32)
        sq = sb("sq", [P, RB, D], f32)
        RW = GPP * GE
        KC = RCH * C
        regA = sb("regA", [P, max(2 * RW, 4 * 2 * GE + 4 * TPG * C + GRING * TPG * H)], f32)
        src_ri = regA[:, 0:RW].bitcast(i32).rearrange("p (b e) -> p b e", e=GE)
        src_rf = regA[:, 0:RW].rearrange("p (b e) -> p b e", e=GE)
        dst_ri = regA[:, RW:2 * RW].bitcast(i32).rearrange("p (b e) -> p b e", e=GE)
        R = regA[:, 0:4 * 2 * GE].rearrange("p (q e) -> p q e", q=UNROLL)
        o1 = 4 * 2 * GE
        scat = regA[:, o1:o1 + 4 * TPG * C].rearrange("p (s t c) -> p s t c", s=4, c=C)
        o2 = o1 + 4 * TPG * C
        X = regA[:, o2:o2 + GRING * TPG * H].rearrange("p (s t f) -> p s t f", s=GRING, f=H)
        regB = sb("regB", [P, max(RB * H, NACC * NSETS * KC)], f32)
        p_sb = regB[:, 0:RB * H].rearrange("p (r f) -> p r f", f=H)
        SA = regB[:, 0:NACC * NSETS * KC].rearrange("p (s k c) -> p s k c", s=NACC, k=NSETS)
        srcH = sb("srcH", [P, GPP, GE], bf16)
        srcL = sb("srcL", [P, GPP, GE], bf16)
        dstR = sb("dstR", [P, GPP, GE], bf16)
        far = sq.rearrange("p r f -> p (r f)")[:, 0:RW // 2].bitcast(bf16)
        srcI = sb("srcI", [P, NT], i32)
        srcF = sb("srcF", [P, NT], f32)
        home = sb("home", [P, NT], f32)
        toscrap = sb("toscrap", [P, NT], f32)
        dstI = sb("dstI", [P, NT], i32)
        base = sb("base", [1, P * GPP], i32)
        L = sb("L", [P, UNROLL, H], f32)
        S = sb("S", [P, 4, TPG, TILE], f32)
        h1 = sb("h1", [P, 2, GE], f32)
        h2 = sb("h2", [P, 2, TPG, C], f32)
        cnt = sb("cnt", [P, UNROLL, TPG], f32)
        extra = sb("extra", [P, 2, TPG], f32)
        idx = sb("idx", [P, UNROLL, TPG], i32)
        gidx = sb("gidx", [P, GRING, TPG], i32)
        zeros = sb("zeros", [P, C * 10], f32)
        ident = sb("ident", [P, P], f32)
        tri = sb("tri", [P, P], f32)
        onesf = sb("onesf", [P, P], f32)
        onesb = sb("onesb", [P, P], bf16)
        sel = sb("sel", [P, P], bf16)
        winrow = sb("winrow", [P, 1], f32)
        oh_row = sb("oh_row", [P, 1], f32)
        scrapc = sb("scrapc", [P, 1], f32)
        epsc = sb("epsc", [P, 1], f32)
        midc = sb("midc", [P, 2], f32)
        tabrow = sb("tabrow", [P, TPG], f32)
        w1x = sb("w1x", [P, 2, H], f32)
        w2 = sb("w2", [H, H], f32)
        wax = sb("wax", [P, 2, H], f32)
        waa = sb("waa", [H, H], f32)
        wau = sb("wau", [DU, H], f32)
        wb = sb("wb", [H, D], f32)
        u0 = sb("u0", [DU, 1], f32)
        b1b = sb("b1b", [P, H], f32)
        b2b = sb("b2b", [P, H], f32)
        b2w = sb("b2w", [P, 2, H], f32)
        b2p = sb("b2p", [P, 3, H], bf16)
        b2R = sb("b2R", [P, TPG, H], bf16)
        bac = sb("bac", [H, 1], f32)
        biasz = sb("biasz", [H, 1], f32)
        bbb = sb("bbb", [P, D], f32)
        stat = sb("stat", [P, 5, RB], f32)
        viol = sb("viol", [P, 6], f32)
        mode = sb("mode", [1, 1], i32)
        rc = sb("rc", [P, 2, RCH], f32)

        def take(width, at=[0]):
            at[0] += width
            return regA[:, at[0] - width:at[0]]

        s2 = take(2 * 2 * KC).rearrange("p (s k) -> p s k", s=2)
        s1 = take(KC)
        agg = take(2 * GE).rearrange("p (s r f) -> p s r f", s=2, f=H)
        aggT = take(2 * GE).rearrange("p (s e) -> p s e", s=2)
        zT = take(2 * GE).rearrange("p (s e) -> p s e", s=2)

        bank = ctx.enter_context(nc.psum_tensor("bank", [P, 8, 512], f32))
        psDst, psSrc = bank[:, 0, :], bank[:, 1, :]

        def psL1(s):
            return bank[:, 2 + s, :]

        def psL2(s):
            return bank[:, 4 + s, :]

        psSum = bank[:, 6:8, 0:2 * C]

        x_in = [sem(f"x_in{n}") for n in range(2)]
        src_rows_in = sem("src_rows_in")
        dst_rows_in = sem("dst_rows_in")
        src_cols_in = sem("src_cols_in")
        dst_cols_in = sem("dst_cols_in")
        base_in = sem("base_in")
        w1_in = sem("w1_in")
        w2_in = sem("w2_in")
        b2_in = sem("b2_in")
        wz_in = sem("wz_in")
        consts = sem("consts")
        zeroed = sem("zeroed")
        sums_zeroed = sem("sums_zeroed")
        dve_step = sem("dve_step")
        act_step = sem("act_step")
        ln_centred = sem("ln_centred")
        ln_squared = sem("ln_squared")
        ln_var = sem("ln_var")
        ln_std = sem("ln_std")
        h_ready = sem("h_ready")
        hT_psum = sem("hT_psum")
        hT_ready = sem("hT_ready")
        p_psum = sem("p_psum")
        p_ready = sem("p_ready")
        table_stored = sem("table_stored")
        far_ready = sem("far_ready")
        viol_sum = sem("viol_sum")
        mode_ready = sem("mode_ready")
        src_high = sem("src_high")
        srcL_ready = sem("srcL_ready")
        dstR_ready = sem("dstR_ready")
        srcF_ready = sem("srcF_ready")
        toscrap_ready = sem("toscrap_ready")
        home_ready = sem("home_ready")
        sel_ready = sem("sel_ready")
        b2_ready = sem("b2_ready")
        xbb_ready = sem("xbb_ready")
        zb_psum = sem("zb_psum")
        biasz_ready = sem("biasz_ready")

        ea_in = [sem(f"ea_in{q}") for q in range(4)]
        win_in = [sem(f"win_in{q}") for q in range(UNROLL)]
        bcast_done = sem("bcast_done")
        oh_ready = sem("oh_ready")
        mask_ready = sem("mask_ready")
        extra_ready = sem("extra_ready")
        idx_ready = sem("idx_ready")
        l1_done = sem("l1_done")
        h1_ready = sem("h1_ready")
        l2_done = sem("l2_done")
        h2_ready = sem("h2_ready")
        sum_done = sem("sum_done")
        scat_ready = sem("scat_ready")
        added = [sem(f"added{k}") for k in range(NSETS)]
        gidx_ready = sem("gidx_ready")
        gathered = [sem(f"gathered{s}") for s in range(GRING)]

        acc_in = [sem(f"acc_in{s}") for s in range(NACC)]
        s2_done = sem("s2_done")
        s1_done = sem("s1_done")
        agg_ready = sem("agg_ready")
        aggT_psum = sem("aggT_psum")
        aggT_ready = sem("aggT_ready")
        z_psum = sem("z_psum")
        z_ready = sem("z_ready")
        o_psum = sem("o_psum")
        o_ready = sem("o_ready")
        stored = sem("stored")

        block = ctx.enter_context(nc.Block())

        def live(i, j):
            return not isinstance(i, int) or 0 <= UNROLL * i + j < NG

        def wait(eng, s, value):
            if not isinstance(value, int) or value > 0:
                eng.wait_ge(s, value)

        def run_steps(eng, step, lead, lag):
            for j in range(-lead, UNROLL):
                step(0, j)
            with eng.Fori(1, STEPS - 1) as i:
                for j in range(UNROLL):
                    step(i, j)
            for j in range(UNROLL + lag):
                step(STEPS - 1, j)

        @block.sync
        def _(sp):
            x_v = x.rearrange("(p r) f -> p r f", p=P)
            for n, (c0, c1) in enumerate(HALVES):
                sp.dma_start(x_sb[:, RCH * c0:RCH * c1, :], x_v[:, RCH * c0:RCH * c1, :]).then_inc(x_in[n], 16)
            sp.dma_start(dst_ri, dst_rows).then_inc(dst_rows_in, 16)
            sp.dma_start(src_ri, src_rows).then_inc(src_rows_in, 16)
            sp.wait_ge(consts, 12)
            for q in range(2):
                sp.dma_start(w1x[q * D:(q + 1) * D, q, :], w1t[0:D, :]).then_inc(w1_in, 16)
            sp.dma_start(b1b[:, :], b1.partition_broadcast(P)).then_inc(w1_in, 16)
            sp.dma_start(L[0:D, :, :], w1t[D:2 * D, :].unsqueeze(1).broadcast_to([D, UNROLL, H])).then_inc(w2_in, 16)
            sp.dma_start(w2[:, :], w2t).then_inc(w2_in, 16)
            with nc.allow_non_contiguous_dma("first dst of each group"):
                sp.dma_start(base[0:1, :], dst_rows[:, :, 0:1].rearrange("(a s) b o -> a (s b o)", a=1)).then_inc(base_in, 16)

            def zero(k):
                sp.dma_start(sums[k * NROWS // 2:(k + 1) * NROWS // 2, :].rearrange("(p a b) c -> p a (b c)", p=P, b=2),
                             zeros[:, 0:2 * C].unsqueeze(1).broadcast_to([P, RB // 4, 2 * C])).then_inc(sums_zeroed, 16)

            def store_p(n):
                c0, c1 = HALVES[n]
                sp.wait_ge(p_ready, c1)
                sp.dma_start(table_v[:, RCH * c0:RCH * c1, :], p_sb[:, RCH * c0:RCH * c1, :]).then_inc(table_stored, 16)

            table_v = table.rearrange("(p r) f -> p r f", p=P)
            sp.wait_ge(zeroed, 1)
            for k in range(5):
                zero(k)
            store_p(0)
            zero(5)
            store_p(1)
            zero(6)
            zero(7)
            sp.wait_ge(srcL_ready, 1)
            sp.wait_ge(dstR_ready, 1)
            sp.wait_ge(base_in, 16)
            sp.wait_ge(w2_in, 32)

            def step(i, j):
                if not live(i, j):
                    return
                g = UNROLL * i + j
                if j % 2 == 0:
                    wait(sp, l1_done, g - UNROLL + 2)
                    sp.dma_start(R[0:D, j:j + 2, :], ea[ds(4 * i + j // 2, 1)].rearrange("o f (q e) -> (o f) q e", q=2)).then_inc(ea_in[j // 2], 16)
                wait(sp, l1_done, g - UNROLL + 1)
                wait(sp, table_stored, 32)
                row = sp.value_load(base[0:1, ds(g, 1)], min_val=0, max_val=N - 1)
                sp.dma_start(L[D:P, j, :], table[ds(row, WIN), :]).then_inc(win_in[j], 16)

            run_steps(sp, step, 0, 0)

            for k in range(NSETS):
                sp.wait_ge(added[k], 16 * -(-(NT - k) // NSETS))
            sums_v = sums.rearrange("(k p r) c -> p k (r c)", k=NSETS, p=P)
            out_v = out.rearrange("(p r) f -> p r f", p=P)
            for c in range(NCH + OLAG):
                if c < NCH:
                    wait(sp, s2_done, c - NACC + 1)
                    sp.dma_start(SA[:, c % NACC, :, :], sums_v[:, :, c * KC:(c + 1) * KC]).then_inc(acc_in[c % NACC], 16)
                if c >= OLAG:
                    n = c - OLAG
                    sp.wait_ge(o_ready, n + 1)
                    sp.dma_start(out_v[:, RCH * n:RCH * (n + 1), :], o_sb[:, RCH * n:RCH * (n + 1), :]).then_inc(stored, 16)
            sp.wait_ge(stored, 16 * NCH)

        @block.gpsimd
        def _(pool):
            nc.gpsimd.memset(ident[:, :], 0.0).then_inc(consts, 1)
            nc.gpsimd.memset(tri[:, :], 1.0).then_inc(consts, 1)
            nc.gpsimd.memset(onesf[:, :], 1.0).then_inc(consts, 1)
            nc.gpsimd.memset(onesb[:, :], 1.0).then_inc(consts, 1)
            nc.gpsimd.memset(h2[:, :, :, H:C], 1.0).then_inc(consts, 1)
            nc.gpsimd.memset(w1x[:, :, :], 0.0).then_inc(consts, 1)
            nc.gpsimd.memset(wax[:, :, :], 0.0).then_inc(consts, 1)
            nc.gpsimd.iota(winrow[:, :], [[0, 1]], base=-D, channel_multiplier=1, allow_small_or_imprecise_dtypes=True).then_inc(consts, 1)
            nc.gpsimd.iota(scrapc[:, :], [[0, 1]], base=SCRAP, channel_multiplier=1, allow_small_or_imprecise_dtypes=True).then_inc(consts, 1)
            nc.gpsimd.iota(tabrow[:, :], [[NROWS, TPG]], base=0, channel_multiplier=0, allow_small_or_imprecise_dtypes=True).then_inc(consts, 1)
            pool.wait_ge(consts, 10)
            nc.gpsimd.affine_select(out=ident[:, :], in_=ident[:, :], compare_op=ALU.not_equal, fill=1.0, base=0,
                                    pattern=[[-1, P]], channel_multiplier=1).then_inc(consts, 1)
            nc.gpsimd.affine_select(out=tri[:, :], in_=tri[:, :], compare_op=ALU.is_ge, fill=0.0, base=0,
                                    pattern=[[-1, P]], channel_multiplier=1).then_inc(consts, 1)
            pool.wait_ge(consts, 12)
            pool.wait_ge(ln_centred, 2)
            pool.wait_ge(wz_in, 16 * 8)
            nc.gpsimd.tensor_tensor(x_sb[:, :, :], x_sb[:, :, :], bbb[:, :].unsqueeze(1).broadcast_to([P, RB, D]), ALU.add).then_inc(xbb_ready, 1)
            pool.wait_ge(src_high, 2)
            nc.gpsimd.tensor_tensor(srcL[:, :, :], src_rf, srcH[:, :, :], ALU.subtract).then_inc(srcL_ready, 1)
            pool.wait_ge(srcF_ready, 1)
            nc.gpsimd.tensor_tensor(home[:, :].rearrange("p (g t) -> p g t", t=TPG), srcF[:, :].rearrange("p (g t) -> p g t", t=TPG),
                                    tabrow[:, :].unsqueeze(1).broadcast_to([P, NG, TPG]), ALU.add).then_inc(home_ready, 1)

            pool.wait_ge(mode_ready, 1)
            pool.wait_ge(table_stored, 32)
            pool.wait_ge(dst_cols_in, 16)
            pool.wait_ge(sums_zeroed, 16 * 2 * NSETS)

            nought = pool.alloc_register("nought")
            bound = pool.alloc_register("bound")
            pool.wait_ge(zeroed, 1)
            pool.reg_load(nought, zeros[0:1, 0:1].bitcast(i32))

            def step(i, j, general):
                if general and live(i, j + GLEAD):
                    s = (j + GLEAD) % GRING
                    n = UNROLL * i + j + GLEAD
                    wait(pool, gathered[s], 16 * TPG * (UNROLL // GRING * i + (j + GLEAD) // GRING))
                    wait(pool, l1_done, n - GRING + 1)
                    nc.gpsimd.tensor_copy(gidx[:, s, :], dstI[:, ds(TPG * n, TPG)]).then_inc(gidx_ready, 1)
                    pool.wait_ge(gidx_ready, n + 1)
                    pool.reg_add(bound, nought, NROWS - 1)
                    for t in range(TPG):
                        nc.gpsimd.indirect_dma_start(out=X[:, s, t, :], out_offset=None, in_=table,
                                                     in_offset=bass.IndirectOffsetOnAxis(ap=gidx[:, s, t:t + 1], axis=0), bounds_check=bound).then_inc(gathered[s], 16)
                if not live(i, j) or j < 0:
                    return
                g = UNROLL * i + j
                for t in range(TPG):
                    k = (TPG * j + t) % NSETS
                    wait(pool, added[k], 16 * (UNROLL * TPG // NSETS * i + (TPG * j + t) // NSETS))
                    if t == 0:
                        pool.wait_ge(idx_ready, g + 1)
                        pool.wait_ge(scat_ready, g + 1)
                    pool.reg_add(bound, nought, NSETS * NROWS - 1)
                    nc.gpsimd.indirect_dma_start(out=sums, out_offset=bass.IndirectOffsetOnAxis(ap=idx[:, j, t:t + 1], axis=0),
                                                 in_=scat[:, j % 4, t, :], in_offset=None, bounds_check=bound,
                                                 compute_op=ALU.add).then_inc(added[k], 16)

            general = pool.value_load(mode[0:1, 0:1], min_val=0, max_val=1)
            with pool.If(general == 0):
                run_steps(pool, lambda i, j: step(i, j, False), 0, 0)
            with pool.If(general == 1):
                run_steps(pool, lambda i, j: step(i, j, True), GLEAD, 0)

            for c in range(NCH):
                s = c % NACC
                pool.wait_ge(acc_in[s], 16 * (c // NACC + 1))
                wait(pool, s1_done, c - 1)
                nc.gpsimd.tensor_tensor(s2[:, c % 2, :], SA[:, s, 0:2, :].rearrange("p k c -> p (k c)"), SA[:, s, 2:4, :].rearrange("p k c -> p (k c)"), ALU.add).then_inc(s2_done, 1)

        @block.scalar
        def _(act):
            act.dma_start(b2b[:, :], b2.partition_broadcast(P)).then_inc(b2_in, 16)
            act.dma_start(srcI[:, :], src_cols).then_inc(src_cols_in, 16)
            act.wait_ge(consts, 12)
            for q in range(2):
                act.dma_start(wax[q * D:(q + 1) * D, q, :], wat[0:D, :]).then_inc(wz_in, 16)
            act.dma_start(waa[:, :], wat[D:D + H, :]).then_inc(wz_in, 16)
            act.dma_start(wau[:, :], wat[D + H:D + H + DU, :]).then_inc(wz_in, 16)
            act.dma_start(wb[:, :], wbt).then_inc(wz_in, 16)
            with nc.allow_non_contiguous_dma("two columns of a float per partition"):
                act.dma_start(u0[:, :], u[0:1, :].rearrange("a k -> k a")).then_inc(wz_in, 16)
                act.dma_start(bac[:, :], ba.rearrange("(k a) -> k a", a=1)).then_inc(wz_in, 16)
            act.dma_start(bbb[:, :], bb.partition_broadcast(P)).then_inc(wz_in, 16)
            act.dma_start(dstI[:, :], dst_cols).then_inc(dst_cols_in, 16)
            act.wait_ge(ln_centred, 1)
            (a0, a1), (a2, a3) = [(RCH * c0, RCH * c1) for c0, c1 in HALVES]
            nc.scalar.activation(sq[:, a0:a1, :], h_sb[:, a0:a1, :], ACT.Square).then_inc(ln_squared, 1)
            act.wait_ge(ln_centred, 2)
            nc.scalar.activation(sq[:, a2:a3, :], h_sb[:, a2:a3, :], ACT.Square).then_inc(ln_squared, 1)
            act.wait_ge(ln_var, 1)
            nc.scalar.activation(stat[:, 2, a0:a1], stat[:, 1, a0:a1], ACT.Sqrt, bias=epsc[:, :], scale=1.0 / D).then_inc(ln_std, 1)
            act.wait_ge(ln_var, 2)
            nc.scalar.activation(stat[:, 2, a2:a3], stat[:, 1, a2:a3], ACT.Sqrt, bias=epsc[:, :], scale=1.0 / D).then_inc(ln_std, 1)
            act.wait_ge(src_rows_in, 16)
            nc.scalar.activation(srcH[:, :, :], src_ri, ACT.Copy).then_inc(src_high, 1)
            act.wait_ge(src_high, 1)
            nc.scalar.activation(src_rf, src_ri, ACT.Copy).then_inc(src_high, 1)
            for c in range(NCH):
                act.wait_ge(hT_psum, c + 1)
                nc.scalar.activation(hT[:, c, :, :], bank[:, c % 2, 0:RCH // 2 * P].rearrange("p (q e) -> p q e", e=P), ACT.Copy).then_inc(hT_ready, 1)
            act.wait_ge(dstR_ready, 1)
            act.wait_ge(zeroed, 4)
            nc.scalar.activation(far, dstR[:, :, :].rearrange("p b e -> p (b e)"), ACT.Abs, bias=midc[:, 0:1]).then_inc(act_step, 1)
            act.wait_ge(act_step, 1)
            nc.scalar.activation(far, far, ACT.Relu, bias=midc[:, 1:2], accum_out=viol[:, 1:2]).then_inc(far_ready, 1)
            act.wait_ge(far_ready, 1)
            act.wait_ge(src_cols_in, 16)
            nc.scalar.activation(srcF[:, :], srcI[:, :], ACT.Copy).then_inc(srcF_ready, 1)
            act.wait_ge(srcF_ready, 1)
            act.wait_ge(consts, 12)
            nc.scalar.activation(toscrap[:, :], srcF[:, :], ACT.Identity, bias=scrapc[:, :], scale=-1.0).then_inc(toscrap_ready, 1)
            act.wait_ge(zb_psum, 1)
            nc.scalar.activation(biasz[:, :], bank[:, 6, 0:1], ACT.Identity, bias=bac[:, :]).then_inc(biasz_ready, 1)

            def step(i, j):
                if live(i, j):
                    g = UNROLL * i + j
                    act.wait_ge(l1_done, g + 1)
                    wait(act, l2_done, g - 1)
                    nc.scalar.activation(h1[:, j % 2, :], psL1(j % 2), ACT.Relu).then_inc(h1_ready, 1)
                if live(i, j - 1):
                    g = UNROLL * i + j - 1
                    act.wait_ge(l2_done, g + 1)
                    wait(act, sum_done, g - 1)
                    nc.scalar.activation(h2[:, (j - 1) % 2, :, 0:H], psL2((j - 1) % 2).rearrange("p (t f) -> p t f", t=TPG), ACT.Relu).then_inc(h2_ready, 1)
                if live(i, j - 2):
                    g = UNROLL * i + j - 2
                    act.wait_ge(sum_done, g + 1)
                    for t in range(TPG):
                        n = TPG * (j - 2 - 4) + t
                        wait(act, added[n % NSETS], 16 * (UNROLL * TPG // NSETS * i + n // NSETS + 1))
                    nc.scalar.activation(scat[:, (j - 2) % 4, :, :].rearrange("p (a t) c -> p a (t c)", a=2), psSum, ACT.Copy).then_inc(scat_ready, 1)

            run_steps(act, step, 0, 2)

            for c in range(NCH + 2):
                if c < NCH:
                    act.wait_ge(aggT_psum, c + 1)
                    if c >= 2:
                        act.wait_ge(z_psum, c - 1)
                    nc.scalar.activation(aggT[:, c % 2, :], bank[:, c % 2, :], ACT.Copy).then_inc(aggT_ready, 1)
                if 1 <= c <= NCH:
                    act.wait_ge(z_psum, c)
                    if c >= 3:
                        act.wait_ge(o_psum, c - 2)
                    nc.scalar.activation(zT[:, (c - 1) % 2, :], bank[:, 2 + (c - 1) % 2, :], ACT.Relu, bias=biasz[:, :]).then_inc(z_ready, 1)

        @block.vector
        def _(dve):
            V = nc.vector
            count = [0]

            def link(ins):
                count[0] += 1
                ins.then_inc(dve_step, 1)
                dve.wait_ge(dve_step, count[0])

            half = (WIN - 1) / 2
            V.memset(zeros[:, :], 0.0).then_inc(zeroed, 1)
            V.memset(epsc[:, :], EPS).then_inc(zeroed, 1)
            V.memset(midc[:, 0:1], -half)
            V.memset(midc[:, 1:2], -half - 0.5).then_inc(zeroed, 1)
            V.memset(viol[:, :], 0.0).then_inc(zeroed, 1)

            for n, (c0, c1) in enumerate(HALVES):
                r0, r1 = RCH * c0, RCH * c1
                dve.wait_ge(x_in[n], 16)
                link(V.tensor_reduce(stat[:, 0, r0:r1], x_sb[:, r0:r1, :], axis=AX.X, op=ALU.add))
                link(V.tensor_scalar(stat[:, 3, r0:r1], stat[:, 0, r0:r1], 1.0 / D, None, ALU.mult))
                V.tensor_tensor(h_sb[:, r0:r1, :], x_sb[:, r0:r1, :], stat[:, 3, r0:r1].unsqueeze(2).broadcast_to([P, r1 - r0, D]), ALU.subtract).then_inc(ln_centred, 1)
            for n, (c0, c1) in enumerate(HALVES):
                r0, r1 = RCH * c0, RCH * c1
                dve.wait_ge(ln_squared, n + 1)
                V.tensor_reduce(stat[:, 1, r0:r1], sq[:, r0:r1, :], axis=AX.X, op=ALU.add).then_inc(ln_var, 1)
            for n, (c0, c1) in enumerate(HALVES):
                r0, r1 = RCH * c0, RCH * c1
                dve.wait_ge(ln_std, n + 1)
                link(V.reciprocal(stat[:, 4, r0:r1], stat[:, 2, r0:r1]))
                V.scalar_tensor_tensor(out=h_sb[:, r0:r1, :], in0=h_sb[:, r0:r1, :], scalar=0.0, in1=stat[:, 4, r0:r1].unsqueeze(2).broadcast_to([P, r1 - r0, D]),
                                       op0=ALU.max, op1=ALU.mult).then_inc(h_ready, 1)
            dve.wait_ge(dst_rows_in, 16)
            V.tensor_tensor(dstR[:, :, :], dst_ri, dst_ri[:, :, 0:1].broadcast_to([P, GPP, GE]), ALU.subtract).then_inc(dstR_ready, 1)
            dve.wait_ge(consts, 12)
            dve.wait_ge(b2_in, 16)
            V.tensor_copy(sel[:, :], ident[:, :]).then_inc(sel_ready, 1)
            link(V.tensor_copy(b2p[:, 0, :], b2b[:, :]))
            link(V.tensor_tensor(b2w[:, 0, :], b2b[:, :], b2p[:, 0, :], ALU.subtract))
            link(V.tensor_copy(b2p[:, 1, :], b2w[:, 0, :]))
            link(V.tensor_tensor(b2w[:, 1, :], b2w[:, 0, :], b2p[:, 1, :], ALU.subtract))
            link(V.tensor_copy(b2p[:, 2, :], b2w[:, 1, :]))
            link(V.tensor_scalar(b2w[:, 0, :], b2p[:, 0, :], ident[:, 0:1], None, ALU.mult))
            link(V.scalar_tensor_tensor(out=b2w[:, 1, :], in0=b2p[:, 1, :], scalar=ident[:, 1:2], in1=b2w[:, 0, :], op0=ALU.mult, op1=ALU.add))
            link(V.scalar_tensor_tensor(out=b2w[:, 0, :], in0=b2p[:, 2, :], scalar=ident[:, 2:3], in1=b2w[:, 1, :], op0=ALU.mult, op1=ALU.add))
            V.tensor_copy(b2R[:, :, :], b2w[:, 0, :].unsqueeze(1).broadcast_to([P, TPG, H])).then_inc(b2_ready, 1)
            dve.wait_ge(w1_in, 48)
            for c in range(NCH):
                dve.wait_ge(p_psum, c + 1)
                V.tensor_tensor(p_sb[:, RCH * c:RCH * (c + 1), :], bank[:, 2 + c % 2, :].rearrange("p (r f) -> p r f", r=RCH),
                                b1b[:, :].unsqueeze(1).broadcast_to([P, RCH, H]), ALU.add).then_inc(p_ready, 1)
            dve.wait_ge(viol_sum, 1)
            link(V.tensor_scalar(viol[:, 2:3], bank[:, 7, 0:1], 0.0, None, ALU.is_gt))
            V.tensor_copy(mode[0:1, 0:1], viol[0:1, 2:3]).then_inc(mode_ready, 1)
            link(V.scalar_tensor_tensor(out=oh_row[:, :], in0=viol[:, 2:3], scalar=-1e6, in1=winrow[:, :], op0=ALU.mult, op1=ALU.add))
            dve.wait_ge(srcF_ready, 1)
            dve.wait_ge(toscrap_ready, 1)
            dve.wait_ge(home_ready, 1)

            def step(i, j):
                if live(i, j):
                    g = UNROLL * i + j
                    dve.wait_ge(bcast_done, g + 1)
                    wait(dve, l1_done, g - UNROLL + 1)
                    V.tensor_scalar(R[D:P, j, :], psDst[D:P, :], oh_row[D:P, :], None, ALU.is_equal).then_inc(oh_ready, 1)
                    wait(dve, sum_done, g - 3)
                    for t in range(TPG):
                        mask = V.scalar_tensor_tensor(out=S[:, j % 4, t, :], in0=psSrc[:, t * TILE:(t + 1) * TILE], scalar=srcF[:, ds(TPG * g + t, 1)],
                                                      in1=tri[:, :], op0=ALU.is_equal, op1=ALU.mult, accum_out=cnt[:, j, t:t + 1])
                    mask.then_inc(mask_ready, 1)
                if live(i, j - 1):
                    g = UNROLL * i + j - 1
                    dve.wait_ge(mask_ready, g + 1)
                    wait(dve, idx_ready, g - 1)
                    V.scalar_tensor_tensor(out=extra[:, (j - 1) % 2, :], in0=cnt[:, (j - 1) % UNROLL, :], scalar=1.5, in1=toscrap[:, ds(TPG * g, TPG)],
                                           op0=ALU.is_gt, op1=ALU.mult).then_inc(extra_ready, 1)
                if live(i, j - 2):
                    g = UNROLL * i + j - 2
                    dve.wait_ge(extra_ready, g + 1)
                    wait(dve, scat_ready, g - 3)
                    V.tensor_tensor(idx[:, (j - 2) % UNROLL, :], extra[:, (j - 2) % 2, :], home[:, ds(TPG * g, TPG)], ALU.add).then_inc(idx_ready, 1)

            run_steps(dve, step, 0, 2)

            dve.wait_ge(xbb_ready, 1)
            for c in range(NCH + 3):
                if c < NCH:
                    dve.wait_ge(s2_done, c + 1)
                    V.tensor_tensor(s1, s2[:, c % 2, 0:KC], s2[:, c % 2, KC:2 * KC], ALU.add).then_inc(s1_done, 1)
                    dve.wait_ge(s1_done, c + 1)
                    s1v = s1.rearrange("p (r c) -> p r c", r=RCH)
                    link(V.tensor_scalar(rc[:, 0, :], s1v[:, :, H], 1.0, None, ALU.max))
                    link(V.reciprocal(rc[:, 1, :], rc[:, 0, :]))
                    wait(dve, aggT_psum, c - 1)
                    V.tensor_tensor(agg[:, c % 2, :, :], s1v[:, :, 0:H], rc[:, 1, :].unsqueeze(2).broadcast_to([P, RCH, H]), ALU.mult).then_inc(agg_ready, 1)
                    dve.wait_ge(agg_ready, c + 1)
                if c >= 3:
                    n = c - 3
                    dve.wait_ge(o_psum, n + 1)
                    V.tensor_tensor(o_sb[:, RCH * n:RCH * (n + 1), :], bank[:, 4 + n % 2, 0:RCH * D].rearrange("p (r f) -> p r f", r=RCH),
                                    x_sb[:, RCH * n:RCH * (n + 1), :], ALU.add).then_inc(o_ready, 1)

        @block.tensor
        def _(pe):
            T = nc.tensor
            pe.wait_ge(consts, 12)
            pe.wait_ge(w1_in, 48)
            for c in range(NCH + 1):
                if c < NCH:
                    for n, (c0, _) in enumerate(HALVES):
                        if c == c0:
                            pe.wait_ge(h_ready, n + 1)
                    if c >= 2:
                        pe.wait_ge(hT_ready, c - 1)
                    for q in range(RCH // 2):
                        r = RCH * c + 2 * q
                        last = T.transpose(bank[:, c % 2, q * P:(q + 1) * P], h_sb[:, r:r + 2, :].rearrange("p r f -> p (r f)"), ident[:, :])
                    last.then_inc(hT_psum, 1)
                if c >= 1:
                    n = c - 1
                    pe.wait_ge(hT_ready, n + 1)
                    if n >= 2:
                        pe.wait_ge(p_ready, n - 1)
                    for q in range(RCH // 2):
                        last = T.matmul(bank[:, 2 + n % 2, 2 * q * H:2 * (q + 1) * H], hT[:, n, q, :], w1x[:, :, :].rearrange("p s f -> p (s f)"), start=True, stop=True)
                    last.then_inc(p_psum, 1)
            pe.wait_ge(far_ready, 1)
            T.matmul(bank[:, 7, 0:1], onesf[:, :], viol[:, 1:2], start=True, stop=True).then_inc(viol_sum, 1)
            pe.wait_ge(wz_in, 16 * 8)
            T.matmul(bank[:, 6, 0:1], wau[:, :], u0[:, :], start=True, stop=True).then_inc(zb_psum, 1)
            pe.wait_ge(sel_ready, 1)
            pe.wait_ge(b2_ready, 1)
            pe.wait_ge(srcL_ready, 1)
            pe.wait_ge(dstR_ready, 1)
            pe.wait_ge(w2_in, 32)
            pe.wait_ge(mode_ready, 1)
            pe.wait_ge(biasz_ready, 1)
            pe.wait_ge(p_ready, NCH)

            def step(i, j, general):
                if live(i, j) and j >= 0:
                    g = UNROLL * i + j
                    pe.wait_ge(oh_ready, g + 1)
                    pe.wait_ge(ea_in[j // 2], 16 * (i + 1))
                    pe.wait_ge(win_in[j], 16 * (i + 1))
                    wait(pe, h1_ready, g - 1)
                    if not general:
                        T.matmul(psL1(j % 2), L[:, j, :], R[:, j, :], start=True, stop=True).then_inc(l1_done, 1)
                    else:
                        T.matmul(psL1(j % 2), L[:, j, :], R[:, j, :], start=True, stop=False)
                        pe.wait_ge(gathered[j % GRING], 16 * TPG * (UNROLL // GRING * i + j // GRING + 1))
                        for t in range(TPG):
                            last = T.matmul(psL1(j % 2)[:, t * TILE:(t + 1) * TILE], X[:, j % GRING, t, :], ident[:, :], start=False, stop=t == TPG - 1)
                        last.then_inc(l1_done, 1)
                if live(i, j - 1) and j - 1 >= -1:
                    g = UNROLL * i + j - 1
                    s = (j - 1) % 2
                    pe.wait_ge(h1_ready, g + 1)
                    wait(pe, h2_ready, g - 1)
                    T.matmul(psL2(s), onesb[:, :], b2R[:, :, :].rearrange("p t f -> p (t f)"), start=True, stop=False)
                    for t in range(TPG):
                        last = T.matmul(psL2(s)[:, t * H:(t + 1) * H], h1[:, s, t * TILE:(t + 1) * TILE], w2[:, :], start=False, stop=t == TPG - 1)
                    last.then_inc(l2_done, 1)
                if live(i, j - 2):
                    g = UNROLL * i + j - 2
                    pe.wait_ge(h2_ready, g + 1)
                    pe.wait_ge(mask_ready, g + 1)
                    wait(pe, scat_ready, g)
                    for t in range(TPG):
                        last = T.matmul(bank[:, 6 + t // 2, (t % 2) * C:(t % 2 + 1) * C], S[:, (j - 2) % 4, t, :], h2[:, (j - 2) % 2, t, :], start=True, stop=True)
                    last.then_inc(sum_done, 1)
                if live(i, j + 2):
                    g = UNROLL * i + j + 2
                    b = (j + 2) % GPP
                    col = UNROLL // GPP * i + (j + 2) // GPP
                    one = sel[:, ds(col, 1)].broadcast_to([P, P])
                    wait(pe, oh_ready, g)
                    T.matmul(psDst, one, dstR[:, b, :], start=True, stop=True)
                    wait(pe, mask_ready, g)
                    T.matmul(psSrc, one, srcH[:, b, :], start=True, stop=False)
                    T.matmul(psSrc, one, srcL[:, b, :], start=False, stop=True).then_inc(bcast_done, 1)

            general = pe.value_load(mode[0:1, 0:1], min_val=0, max_val=1)
            with pe.If(general == 0):
                run_steps(pe, lambda i, j: step(i, j, False), 2, 2)
            with pe.If(general == 1):
                run_steps(pe, lambda i, j: step(i, j, True), 2, 2)

            pe.wait_ge(scat_ready, NG)
            for c in range(NCH + 2):
                if c < NCH:
                    pe.wait_ge(agg_ready, c + 1)
                    if c >= 2:
                        pe.wait_ge(aggT_ready, c - 1)
                    for r in range(RCH):
                        last = T.transpose(bank[:, c % 2, r * P:(r + 1) * P], agg[:, c % 2, r, :], ident[:, :])
                    last.then_inc(aggT_psum, 1)
                if 1 <= c <= NCH:
                    n = c - 1
                    pe.wait_ge(aggT_ready, n + 1)
                    if n >= 2:
                        pe.wait_ge(z_ready, n - 1)
                    T.matmul(bank[:, 2 + n % 2, :], waa[:, :], aggT[:, n % 2, :], start=True, stop=False)
                    for s in range(2):
                        z_half = bank[:, 2 + n % 2, :].rearrange("p (q s e) -> p q s e", q=RCH // 2, s=2)[:, :, s, :]
                        last = T.matmul(z_half, wax[:, s, :], hT[:, n, :, :], start=False, stop=s == 1)
                    last.then_inc(z_psum, 1)
                if c >= 2:
                    n = c - 2
                    pe.wait_ge(z_ready, n + 1)
                    if n >= 2:
                        pe.wait_ge(o_ready, n - 1)
                    for r in range(RCH):
                        last = T.matmul(bank[:, 4 + n % 2, r * D:(r + 1) * D], zT[:, n % 2, r * P:(r + 1) * P], wb[:, :], start=True, stop=True)
                    last.then_inc(o_psum, 1)


def kernel(x, src, dst, edge_attr_64, L0_gnn_u, L0_gnn_W1, L0_gnn_b1, L0_gnn_W2, L0_gnn_b2, L0_gnn_Wa, L0_gnn_ba, L0_gnn_Wb, L0_gnn_bb):
    import numpy as np
    import concourse.bacc as bacc
    from concourse.bass_utils import run_bass_kernel_spmd

    def pad(a, n, fill):
        a = np.asarray(a)
        return np.concatenate([a, np.full((n - a.shape[0],) + a.shape[1:], fill, a.dtype)])

    rows = P * GPP * GE
    src_p = pad(src, rows, NROWS - 1)
    dst_p = pad(dst, rows, N - 1)
    arrays = {
        "x": pad(x, NROWS, 0),
        "src_cols": np.ascontiguousarray(src_p[:NT * TILE].reshape(NT, TILE).T),
        "dst_cols": np.ascontiguousarray(dst_p[:NT * TILE].reshape(NT, TILE).T),
        "src_rows": src_p.reshape(P, GPP, GE),
        "dst_rows": dst_p.reshape(P, GPP, GE),
        "ea": np.ascontiguousarray(pad(edge_attr_64, PAIRS * 2 * GE, 0).reshape(PAIRS, 2 * GE, D).transpose(0, 2, 1)),
        "u": np.asarray(L0_gnn_u),
        "w1t": np.ascontiguousarray(np.asarray(L0_gnn_W1).T),
        "b1": np.asarray(L0_gnn_b1),
        "w2t": np.ascontiguousarray(np.asarray(L0_gnn_W2).T),
        "b2": np.asarray(L0_gnn_b2),
        "wat": np.ascontiguousarray(np.asarray(L0_gnn_Wa).T),
        "ba": np.asarray(L0_gnn_ba),
        "wbt": np.ascontiguousarray(np.asarray(L0_gnn_Wb).T),
        "bb": np.asarray(L0_gnn_bb),
    }
    nc = bacc.Bacc("TRN2", target_bir_lowering=False, num_devices=1)
    args = {}
    for name, a in arrays.items():
        args[name] = nc.dram_tensor(f"in_{name}", a.shape, mybir.dt.from_np(a.dtype), kind="ExternalInput").ap()
    out = nc.dram_tensor("out", (NROWS, D), mybir.dt.float32, kind="ExternalOutput").ap()
    build(nc, out=out, **args)
    r = run_bass_kernel_spmd(nc, [{f"in_{name}": a for name, a in arrays.items()}], core_ids=[0])
    return r.results[0]["out"][:N]
```
